# Optimizing a Trainium2 kernel written in Bass

```python
import numpy as np
import jax
import jax.numpy as jnp

def _softmax(x, axis=-1):
    return jax.nn.softmax(x, axis=axis)

def _gelu(x):
    return jax.nn.gelu(x, approximate=True)

def _silu(x):
    return jax.nn.silu(x)

def _sigmoid(x):
    return jax.nn.sigmoid(x)

def _layernorm(x, axis=-1, eps=1e-05):
    m = jnp.mean(x, axis=axis, keepdims=True)
    v = jnp.var(x, axis=axis, keepdims=True)
    return (x - m) / jnp.sqrt(v + eps)

def _scatter_add(tgt, idx, src, axis=0):
    return tgt.at[idx].add(src)

def _segment_sum(src, seg, n):
    return jax.ops.segment_sum(src, seg, n)
kernel_name = 'mk_recurrent_d1_jaxref_r8_1856e0'

def setup_inputs(seed: int=0):
    np.random.seed(seed)
    _w = jnp.asarray

    def _L0_attn_setup():
        import math
        import jax, jax.numpy as jnp
        import numpy as np
        N_HEADS = 32
        ALIBI_BIAS_MAX = 8

        def _alibi_slopes(n_heads, alibi_bias_max=8):
            _n = 2 ** math.ceil(math.log2(n_heads))
            m = jnp.arange(1, _n + 1, dtype=jnp.float32) * (alibi_bias_max / _n)
            slopes = 1.0 / jnp.power(2.0, m)
            if _n != n_heads:
                slopes = jnp.concatenate([slopes[1::2], slopes[::2]])[:n_heads]
            return slopes
        key = jax.random.key(seed)
        k1, k2, k3 = jax.random.split(key, 3)
        B, S, D = (1, 256, 512)
        x = jax.random.normal(k1, (B, S, D), dtype=jnp.float32)
        w_qkv = jax.random.normal(k2, (3 * D, D), dtype=jnp.float32) * 0.02
        b_qkv = jnp.zeros((3 * D,), dtype=jnp.float32)
        w_out = jax.random.normal(k3, (D, D), dtype=jnp.float32) * 0.02
        b_out = jnp.zeros((D,), dtype=jnp.float32)
        return {'x': x, 'w_qkv': w_qkv, 'b_qkv': b_qkv, 'w_out': w_out, 'b_out': b_out}
    _L0_attn_in = _L0_attn_setup()

    def _L0_ffn_setup():
        import jax, jax.numpy as jnp
        import numpy as np
        _TRIPLES = [(1, 2, 3), (1, 4, 5), (1, 7, 6), (2, 4, 6), (2, 5, 7), (3, 4, 7), (3, 6, 5)]

        def _oct_struct():
            S = np.zeros((8, 8, 8), np.float32)
            S[0, 0, 0] = 1.0
            for i in range(1, 8):
                S[0, i, i] = 1.0
                S[i, 0, i] = 1.0
                S[i, i, 0] = -1.0
            for a, b, c in _TRIPLES:
                for x, y, z in ((a, b, c), (b, c, a), (c, a, b)):
                    S[x, y, z] = 1.0
                    S[y, x, z] = -1.0
            return jnp.asarray(S)
        S_OCT = _oct_struct()
        N_EMBD = 512
        HIDDEN = 1366

        def ternary_dequant(W):
            scale = jnp.mean(jnp.abs(W))
            Wq = scale * jnp.clip(jnp.round(W / scale), -1.0, 1.0)
            return W + jax.lax.stop_gradient(Wq - W)

        def oct_ternary_linear(xp, W):
            Wq = ternary_dequant(W)
            M = jnp.einsum('jik,jod->koid', S_OCT, Wq)
            return jnp.einsum('...id,koid->...ko', xp, M)
        key = jax.random.key(seed)
        k1, k2, k3, k4 = jax.random.split(key, 4)
        B, T = (2, 256)
        d8, h8 = (N_EMBD // 8, HIDDEN // 8)
        std_in = 1.0 / np.sqrt(N_EMBD)
        std_h = 1.0 / np.sqrt(HIDDEN)
        return {'x': jax.random.normal(k1, (B, T, N_EMBD), jnp.float32), 'w_gate': jax.random.normal(k2, (8, h8, d8), jnp.float32) * std_in, 'w_up': jax.random.normal(k3, (8, h8, d8), jnp.float32) * std_in, 'w_down': jax.random.normal(k4, (8, d8, h8), jnp.float32) * std_h}
    _L0_ffn_in = _L0_ffn_setup()
    _d = {'L0_attn_x': _L0_attn_in['x'], 'L0_attn_w_qkv': _L0_attn_in['w_qkv'], 'L0_attn_b_qkv': _L0_attn_in['b_qkv'], 'L0_attn_w_out': _L0_attn_in['w_out'], 'L0_attn_b_out': _L0_attn_in['b_out'], 'L0_ffn_w_gate': _L0_ffn_in['w_gate'], 'L0_ffn_w_up': _L0_ffn_in['w_up'], 'L0_ffn_w_down': _L0_ffn_in['w_down']}
    _x0 = _d['L0_attn_x']
    _d['L0_attn_x'] = jax.random.normal(jax.random.fold_in(jax.random.key(seed), 1), (2, 1024, 512), dtype=_x0.dtype)
    del _x0
    return _d

def reference(L0_attn_x, L0_attn_w_qkv, L0_attn_b_qkv, L0_attn_w_out, L0_attn_b_out, L0_ffn_w_gate, L0_ffn_w_up, L0_ffn_w_down):

    def _L0_attn_ref(x, w_qkv, b_qkv, w_out, b_out):
        import math
        import jax, jax.numpy as jnp
        import numpy as np
        N_HEADS = 32
        ALIBI_BIAS_MAX = 8

        def _alibi_slopes(n_heads, alibi_bias_max=8):
            _n = 2 ** math.ceil(math.log2(n_heads))
            m = jnp.arange(1, _n + 1, dtype=jnp.float32) * (alibi_bias_max / _n)
            slopes = 1.0 / jnp.power(2.0, m)
            if _n != n_heads:
                slopes = jnp.concatenate([slopes[1::2], slopes[::2]])[:n_heads]
            return slopes
        B, S, D = x.shape
        H = N_HEADS
        hd = D // H
        qkv = jnp.einsum('bsd,od->bso', x, w_qkv) + b_qkv
        q, k, v = jnp.split(qkv, 3, axis=-1)
        q = q.reshape(B, S, H, hd)
        k = k.reshape(B, S, H, hd)
        v = v.reshape(B, S, H, hd)
        scale = 1.0 / math.sqrt(hd)
        scores = jnp.einsum('bqhd,bkhd->bhqk', q, k) * scale
        slopes = _alibi_slopes(H, ALIBI_BIAS_MAX)
        positions = jnp.arange(1 - S, 1, dtype=jnp.float32)
        alibi = slopes[:, None] * positions[None, :]
        scores = scores + alibi[None, :, None, :]
        causal = jnp.arange(S)[:, None] >= jnp.arange(S)[None, :]
        scores = jnp.where(causal[None, None, :, :], scores, jnp.float32(-1000000000.0))
        attn = jax.nn.softmax(scores, axis=-1)
        out = jnp.einsum('bhqk,bkhd->bqhd', attn, v).reshape(B, S, D)
        return jnp.einsum('bsd,od->bso', out, w_out) + b_out

    def _L0_ffn_ref(x, w_gate, w_up, w_down):
        import jax, jax.numpy as jnp
        import numpy as np
        _TRIPLES = [(1, 2, 3), (1, 4, 5), (1, 7, 6), (2, 4, 6), (2, 5, 7), (3, 4, 7), (3, 6, 5)]

        def _oct_struct():
            S = np.zeros((8, 8, 8), np.float32)
            S[0, 0, 0] = 1.0
            for i in range(1, 8):
                S[0, i, i] = 1.0
                S[i, 0, i] = 1.0
                S[i, i, 0] = -1.0
            for a, b, c in _TRIPLES:
                for x, y, z in ((a, b, c), (b, c, a), (c, a, b)):
                    S[x, y, z] = 1.0
                    S[y, x, z] = -1.0
            return jnp.asarray(S)
        S_OCT = _oct_struct()
        N_EMBD = 512
        HIDDEN = 1366

        def ternary_dequant(W):
            scale = jnp.mean(jnp.abs(W))
            Wq = scale * jnp.clip(jnp.round(W / scale), -1.0, 1.0)
            return W + jax.lax.stop_gradient(Wq - W)

        def oct_ternary_linear(xp, W):
            Wq = ternary_dequant(W)
            M = jnp.einsum('jik,jod->koid', S_OCT, Wq)
            return jnp.einsum('...id,koid->...ko', xp, M)
        B, T, D = x.shape
        xp = x.reshape(B, T, 8, D // 8)
        gate = oct_ternary_linear(xp, w_gate).reshape(B, T, -1)
        up = oct_ternary_linear(xp, w_up).reshape(B, T, -1)
        h = jax.nn.silu(gate) * up
        hp = h.reshape(B, T, 8, h.shape[-1] // 8)
        out = oct_ternary_linear(hp, w_down).reshape(B, T, D)
        return out
    x = L0_attn_x
    xn = _layernorm(x, axis=-1)
    s = _L0_attn_ref(xn, L0_attn_w_qkv, L0_attn_b_qkv, L0_attn_w_out, L0_attn_b_out)
    g = _silu(_L0_ffn_ref(xn, L0_ffn_w_gate, L0_ffn_w_up, L0_ffn_w_down))
    x = x + s * g
    return x

_drawn_inputs = setup_inputs


def setup_inputs(seed=0):
    import zlib

    import numpy as np

    out = dict(_drawn_inputs(seed))
    spreads = {'L0_attn_b_qkv': (0.0, 0.8), 'L0_attn_b_out': (0.0, 0.8)}
    factors = {'L0_attn_w_qkv': 8.0,
     'L0_attn_w_out': 8.0,
     'L0_ffn_w_gate': 5.778,
     'L0_ffn_w_up': 5.581,
     'L0_ffn_w_down': 5.571}
    for name, (base, spread) in spreads.items():
        noise = np.random.default_rng([zlib.crc32(name.encode()), seed]).standard_normal(out[name].shape)
        drawn = base * np.exp(spread * noise) if base else spread * noise
        out[name] = jnp.asarray(drawn.astype(out[name].dtype))
    for name, factor in factors.items():
        out[name] = (out[name] * factor).astype(out[name].dtype)
    return out
```

```python
import concourse.bass as bass
from concourse import mybir
from contextlib import ExitStack

B, S, D, H = 2, 1024, 512, 32
HD = D // H
T = B * S
P = 128
KT = D // P
CH = 512
NCH = T // CH
TT = CH // P
OC = 8
HO, DO = 1366 // OC, D // OC
HID = OC * HO
HT = -(-HID // P)
GRP = HO // 2
EPS = 1e-5
TRIPLES = [(1, 2, 3), (1, 4, 5), (1, 7, 6), (2, 4, 6), (2, 5, 7), (3, 4, 7), (3, 6, 5)]

QH = 4
NQ = H // QH
QUADS = B * NQ
KB = S // P
TERM_Q = [0, 0, 1, 1, 0, 2]
TERM_K = [0, 1, 0, 1, 2, 0]
ROWS_QK = HD * len(TERM_Q)
ROWS_MAX = ROWS_QK + 3
ROWS_ALL = ROWS_MAX + 3
SLOTS = 3
INV_SCALE = 4.0
MASKED = -1.0e9 * INV_SCALE

X_SCALE = 256.0
H_SCALE = 2.0 ** -19


def octonion():
    by = [[None] * OC for _ in range(OC)]
    by[0][0] = (0, 1.0)
    for i in range(1, OC):
        by[i][i] = (0, 1.0)
        by[i][0] = (i, 1.0)
        by[0][i] = (i, -1.0)
    for a, b, c in TRIPLES:
        for x, y, z in ((a, b, c), (b, c, a), (c, a, b)):
            by[z][y] = (x, 1.0)
            by[z][x] = (y, -1.0)
    return by


OCT = octonion()

QK0, V0, GU0, DN0 = 0, 2 * KT, 2 * KT + TT, 2 * KT + TT + 2 * HT
TILES = DN0 + TT
LN_AT = [1, 2, 3, 6, 7]
RING = 6


def hidden_rows(t):
    return min(P, HID - t * P)


def max_tiles():
    out = []
    for half in range(2):
        for qb in range(4 * half, KB):
            keys = min(CH, P * (qb + 1) - CH * half)
            n = CH // keys
            for h in range(0, QH, n):
                out.append((qb, h, min(n, QH - h), CH * half, keys))
    return out


MAXT = max_tiles()
NMAX = len(MAXT)
STEPS = [(c, kb) for c in range(S // CH) for kb in range(4 * (c + 1))]
NST = len(STEPS)
DIAG = [kb >= 4 * c for c, kb in STEPS]
LEAD = 10
LAG = 2
PSLOTS = 3


def program(nc, x, w_qkv, b_qkv, w_out, b_out, w_gate, w_up, w_down, alibi, out):
    f32, f32r, bf16, f16 = mybir.dt.float32, mybir.dt.float32r, mybir.dt.bfloat16, mybir.dt.float16
    ALU, ACT, AX = mybir.AluOpType, mybir.ActivationFunctionType, mybir.AxisListType

    q_scr = nc.dram_tensor("q_scr", [B, 3, D, S], bf16, kind="Internal").ap()
    k_scr = nc.dram_tensor("k_scr", [B, 3, D, S], bf16, kind="Internal").ap()
    v_scr = nc.dram_tensor("v_scr", [T, D], f32, kind="Internal").ap()
    g_scr = nc.dram_tensor("g_scr", [T, D], f32, kind="Internal").ap()
    o_scr = nc.dram_tensor("o_scr", [B, 2, NQ, P, CH], f32, kind="Internal").ap()

    xf = x.rearrange("b s d -> (b s) d")
    outf = out.rearrange("b s d -> (b s) d")

    top = ExitStack()
    with top:
        def alloc(stack, name, shape, dt):
            return stack.enter_context(nc.sbuf_tensor(name, shape, dt))

        def sem(name):
            return top.enter_context(nc.semaphore(name))

        psum = top.enter_context(nc.psum_tensor("psum", [P, 8, CH], f32))
        banks = [psum[:, i, :] for i in range(8)]
        identf = alloc(top, "identf", [P, P], f32)
        identb = alloc(top, "identb", [P, P], bf16)
        causal = alloc(top, "causal", [P, P], bf16)
        ones = alloc(top, "ones", [P, P], f32)
        OH = alloc(top, "OH", [P, KT, D], f32r)
        OL = alloc(top, "OL", [P, KT, D], f32r)
        bo_row = alloc(top, "bo_row", [P, D], f32)

        one = ExitStack()
        with one:
            WH = alloc(one, "WH", [P, KT, 3 * D], f32r)
            WL = alloc(one, "WL", [P, KT, 3 * D], f32r)
            MG = alloc(one, "MG", [P, KT, 2, HID], f16)
            MD = alloc(one, "MD", [P, HT, D], f16)
            XH = alloc(one, "XH", [P, KT, CH], f32r)
            XL = alloc(one, "XL", [P, KT, CH], f32r)
            X16H = alloc(one, "X16H", [P, KT, CH], f16)
            X16L = alloc(one, "X16L", [P, KT, CH], f16)
            xin = alloc(one, "xin", [P, TT, D], f32)
            stats = alloc(one, "stats", [P, TT, 6], f32)
            moments = alloc(one, "moments", [P, TT, 2], f32)
            var_eps = alloc(one, "var_eps", [P, TT], f32)
            std = alloc(one, "std", [P, TT], f32)
            rstd0 = alloc(one, "rstd0", [P, TT], f32)
            rstd = alloc(one, "rstd", [P, TT], f32)
            newton = alloc(one, "newton", [P, 2, TT], f32)
            bq_col = alloc(one, "bq_col", [P, 2 * KT], f32)
            bv_row = alloc(one, "bv_row", [P, D], f32)
            asum = alloc(one, "asum", [P, 3], f32)
            mean = alloc(one, "mean", [P, 3], f32)
            half = alloc(one, "half", [P, 3], f32)
            nhalf = alloc(one, "nhalf", [P, 3], f32)
            sig_scale = alloc(one, "sig_scale", [P, 1], f32)
            gu_scale = alloc(one, "gu_scale", [P, 1], f32)
            ffn_scale = alloc(one, "ffn_scale", [P, 1], f32)

            s_const = sem("s_const")
            x_loaded = sem("x_loaded")
            wqkv_loaded = [sem(f"wqkv_loaded{i}") for i in range(3)]
            wout_loaded = sem("wout_loaded")
            ffn_loaded = sem("ffn_loaded")
            bias_loaded = sem("bias_loaded")
            ln_step = sem("ln_step")
            std_done = sem("std_done")
            xt_done = sem("xt_done")
            xh_done = sem("xh_done")
            xl_done = sem("xl_done")
            wt_done = sem("wt_done")
            wh_done = sem("wh_done")
            wl_done = sem("wl_done")
            dve_prep = sem("dve_prep")
            asum_done = sem("asum_done")
            mean_ready = sem("mean_ready")
            tern_gu = sem("tern_gu")
            tern_dn = sem("tern_dn")
            tt_done = sem("tt_done")
            tt_copied = sem("tt_copied")
            mg_done = sem("mg_done")
            mdn_done = sem("mdn_done")
            mdt_done = sem("mdt_done")
            md_done = sem("md_done")
            tile_done = sem("tile_done")
            evac_done = sem("evac_done")
            q1_done = sem("q1_done")
            q2_done = sem("q2_done")
            q3_done = sem("q3_done")
            sig_done = sem("sig_done")
            hh_done = sem("hh_done")
            hl_done = sem("hl_done")
            qk_stored = [sem(f"qk_stored{i}") for i in range(2)]
            v_stored = [sem(f"v_stored{i}") for i in range(2)]
            g_stored = [sem(f"g_stored{i}") for i in range(2)]

            XLN = 4 + 4 + 1 + 4 + 4
            NWT = 4 * KT
            NTT = 4

            def normalise(dve, c, stage):
                base = c * XLN
                if stage == 0:
                    dve.wait_ge(x_loaded, c * 16 + 16)
                    for t in range(TT):
                        nc.vector.bn_stats(stats[:, t, :], xin[:, t, :]).then_inc(ln_step, 1)
                if stage == 1:
                    for t in range(TT):
                        nc.vector.bn_aggr(moments[:, t, :], stats[:, t, :]).then_inc(ln_step, 1)
                if stage == 2:
                    dve.wait_ge(ln_step, base + 8)
                    nc.vector.tensor_scalar(var_eps[:], moments[:, :, 1], EPS, None, ALU.add).then_inc(ln_step, 1)
                if stage == 3:
                    dve.wait_ge(std_done, c + 1)
                    nc.vector.reciprocal(rstd0[:], std[:]).then_inc(ln_step, 1)
                    dve.wait_ge(ln_step, base + 10)
                    nc.vector.tensor_tensor(newton[:, 0], var_eps[:], rstd0[:], ALU.mult).then_inc(ln_step, 1)
                    dve.wait_ge(ln_step, base + 11)
                    nc.vector.scalar_tensor_tensor(out=newton[:, 1], in0=newton[:, 0], scalar=-0.5, in1=rstd0[:],
                                                   op0=ALU.mult, op1=ALU.mult).then_inc(ln_step, 1)
                    dve.wait_ge(ln_step, base + 12)
                    nc.vector.scalar_tensor_tensor(out=rstd[:], in0=newton[:, 1], scalar=1.5, in1=rstd0[:],
                                                   op0=ALU.add, op1=ALU.mult).then_inc(ln_step, 1)
                if stage == 4:
                    dve.wait_ge(ln_step, base + 13)
                    for t in range(TT):
                        nc.vector.tensor_scalar(xin[:, t, :], xin[:, t, :], moments[:, t, 0:1], rstd[:, t:t + 1],
                                                ALU.subtract, ALU.mult).then_inc(ln_step, 1)

            def root(act, c):
                act.wait_ge(ln_step, c * XLN + 9)
                nc.scalar.activation(std[:], var_eps[:], ACT.Sqrt).then_inc(std_done, 1)

            prep = ExitStack()
            with prep:
                wnat = alloc(prep, "wnat", [P, 3 * KT, D], f32)
                wonat = alloc(prep, "wonat", [P, KT, D], f32)
                GN = alloc(prep, "GN", [GRP, 2, 2, OC, DO], f32)
                DN = alloc(prep, "DN", [P, OC, HO], f32)
                gtern = alloc(prep, "gtern", [GRP, 2, 2, OC, DO], bf16)
                dtern = alloc(prep, "dtern", [P, OC, HO], bf16)
                TTs = alloc(prep, "TTs", [P, 2, OC, HO], bf16)
                MDn = alloc(prep, "MDn", [P, OC // 2, OC, HO], bf16)
                dneg = TTs[:, 0]
                gneg = TTs[0:GRP, 1].rearrange("p j o -> p (j o)")[:, 0:2 * OC * DO]

                block = prep.enter_context(nc.Block())

                @block.sync
                def _(sp):
                    sp.dma_start(xin[:], xf[0:CH, :].rearrange("(t p) d -> p t d", p=P)).then_inc(x_loaded, 16)
                    for og in range(3):
                        sp.dma_start(wnat[:, og * KT:(og + 1) * KT, :],
                                     w_qkv[og * D:(og + 1) * D, :].rearrange("(t p) d -> p t d", p=P)
                                     ).then_inc(wqkv_loaded[og], 16)
                    sp.dma_start(wonat[:], w_out.rearrange("(t p) d -> p t d", p=P)).then_inc(wout_loaded, 16)

                @block.gpsimd
                def _(pool):
                    for w, src in enumerate((w_gate, w_up)):
                        for g in range(2):
                            pool.dma_start(GN[:, w, g], src[:, g * GRP:(g + 1) * GRP, :].rearrange("j p d -> p j d")
                                           ).then_inc(ffn_loaded, 16)
                    for r in range(2):
                        pool.dma_start(DN[DO * r:DO * (r + 1)], w_down.rearrange("j o d -> o j d")).then_inc(ffn_loaded, 16)
                    pool.dma_start(bq_col[:], b_qkv[0:2 * D].rearrange("(t p) -> p t", p=P),
                                   allow_slow_non_contiguous=True).then_inc(bias_loaded, 16)
                    pool.dma_start(bv_row[:], b_qkv[2 * D:3 * D].partition_broadcast(P)).then_inc(bias_loaded, 16)
                    pool.dma_start(bo_row[:], b_out.partition_broadcast(P)).then_inc(bias_loaded, 16)
                    nc.gpsimd.memset(identf[:], 0.0).then_inc(s_const, 1)
                    nc.gpsimd.memset(identb[:], 0.0).then_inc(s_const, 1)
                    nc.gpsimd.memset(causal[:], 0.0).then_inc(s_const, 1)
                    nc.gpsimd.memset(ones[:], 1.0).then_inc(s_const, 1)
                    pool.wait_ge(s_const, 4)
                    nc.gpsimd.affine_select(out=identf[:], in_=identf[:], compare_op=ALU.not_equal, fill=1.0, base=0,
                                            pattern=[[-1, P]], channel_multiplier=1).then_inc(s_const, 1)
                    nc.gpsimd.affine_select(out=identb[:], in_=identb[:], compare_op=ALU.not_equal, fill=1.0, base=0,
                                            pattern=[[-1, P]], channel_multiplier=1).then_inc(s_const, 1)
                    nc.gpsimd.affine_select(out=causal[:], in_=causal[:], compare_op=ALU.is_ge, fill=MASKED, base=0,
                                            pattern=[[-1, P]], channel_multiplier=1).then_inc(s_const, 1)
                    nc.gpsimd.memset(half[:], 0.0).then_inc(evac_done, TILES)
                    pool.wait_ge(tern_dn, 1)
                    for k in range(OC):
                        for i in range(OC):
                            j, sign = OCT[k][i]
                            rows = slice(DO * (k % 2), DO * (k % 2 + 1))
                            last = nc.gpsimd.tensor_scalar(MDn[rows, k // 2, i, :], dtern[rows, j, :], sign, None, ALU.mult)
                    last.then_inc(mdn_done, 1)

                @block.tensor
                def _(pe):
                    pe.wait_ge(s_const, 7)
                    pe.wait_ge(ln_step, XLN)
                    for kt in range(KT):
                        if kt >= 2:
                            pe.wait_ge(xl_done, 2 * (kt - 1))
                        for t in range(TT):
                            last = nc.tensor.transpose(banks[kt % 2][:, t * P:(t + 1) * P], xin[:, t, kt * P:(kt + 1) * P], identf[:])
                        last.then_inc(xt_done, 1)
                    for n in range(NWT):
                        og, kt = divmod(n, KT)
                        if kt == 0:
                            pe.wait_ge(wqkv_loaded[og] if og < 3 else wout_loaded, 16)
                        if n >= RING:
                            pe.wait_ge(wl_done, n - RING + 1)
                        for t in range(TT):
                            src = wnat[:, og * KT + t, kt * P:(kt + 1) * P] if og < 3 else wonat[:, t, kt * P:(kt + 1) * P]
                            last = nc.tensor.transpose(banks[2 + n % RING][:, t * P:(t + 1) * P], src, identf[:])
                        last.then_inc(wt_done, 1)
                    pe.wait_ge(asum_done, 3)
                    pe.wait_ge(xl_done, 2 * KT)
                    nc.tensor.matmul(banks[0][:, 0:3], ones[:], asum[:], start=True, stop=True).then_inc(mean_ready, 1)
                    pe.wait_ge(tern_gu, 2)
                    pe.wait_ge(wl_done, NWT)
                    for n in range(NTT):
                        w, jq = divmod(n, 2)
                        dst = banks[2 + n][:].bitcast(bf16)
                        for jj in range(OC // 2):
                            for g in range(2):
                                at = (jj * 2 + g) * (GRP + 1)
                                for r in range(2):
                                    last = nc.tensor.transpose(dst[DO * r:DO * (r + 1), at:at + GRP],
                                                               gtern[:, w, g, jq * (OC // 2) + jj, :], identb[0:GRP, 0:GRP])
                        last.then_inc(tt_done, 1)
                    pe.wait_ge(mdn_done, 1)
                    pe.wait_ge(tt_copied, NTT)
                    mdn = MDn[:].rearrange("p k i d -> p k (i d)")
                    for t in range(HT):
                        if t >= RING:
                            pe.wait_ge(md_done, t - RING + 1)
                        dst = banks[2 + t % RING][:].bitcast(bf16)
                        for k in range(OC // 2):
                            last = nc.tensor.transpose(dst[0:hidden_rows(t), k * P:(k + 1) * P],
                                                       mdn[:, k, t * P:t * P + hidden_rows(t)], identb[:])
                        last.then_inc(mdt_done, 1)

                @block.scalar
                def _(act):
                    root(act, 0)
                    for kt in range(KT):
                        act.wait_ge(xt_done, kt + 1)
                        nc.scalar.activation(XH[:, kt, :], banks[kt % 2][:], ACT.Identity).then_inc(xh_done, 1)
                        nc.scalar.activation(X16H[:, kt, :], banks[kt % 2][:], ACT.Identity, scale=X_SCALE).then_inc(xh_done, 1)
                    for n in range(NWT):
                        og, kt = divmod(n, KT)
                        act.wait_ge(wt_done, n + 1)
                        dst = WH[:, kt, og * D:(og + 1) * D] if og < 3 else OH[:, kt, :]
                        nc.scalar.activation(dst, banks[2 + n % RING][:], ACT.Identity).then_inc(wh_done, 1)
                    for n in range(NTT):
                        w, jq = divmod(n, 2)
                        act.wait_ge(tt_done, n + 1)
                        src = banks[2 + n][:].bitcast(bf16)[:, 0:OC * (GRP + 1)].rearrange("p (j g o) -> p j g o", g=2, o=GRP + 1)
                        nc.scalar.activation(TTs[:, w, jq * (OC // 2):(jq + 1) * (OC // 2), :].rearrange("p j (g o) -> p j g o", g=2),
                                             src[:, :, :, 0:GRP], ACT.Identity).then_inc(tt_copied, 1)
                    act.wait_ge(tt_copied, NTT)
                    for k in range(OC):
                        for i in range(0, OC, 2):
                            j, sign = OCT[k][i]
                            last = nc.scalar.mul(MG[0:DO, i // 2, :, k * HO:(k + 1) * HO], TTs[0:DO, :, j, :], sign)
                    last.then_inc(mg_done, 1)
                    for t in range(HT):
                        act.wait_ge(mdt_done, t + 1)
                        rows = hidden_rows(t)
                        nc.scalar.activation(MD[0:rows, t, :], banks[2 + t % RING][0:rows, :].bitcast(bf16)[:, 0:D],
                                             ACT.Identity).then_inc(md_done, 1)

                @block.vector
                def _(dve):
                    chain = [0]

                    def link(ins):
                        chain[0] += 1
                        ins.then_inc(dve_prep, 1)
                        dve.wait_ge(dve_prep, chain[0])

                    nc.vector.memset(asum[:], 0.0).then_inc(asum_done, 1)
                    for stage in range(5):
                        if stage == 1:
                            dve.wait_ge(ln_step, 4)
                        normalise(dve, 0, stage)
                    for kt in range(KT):
                        dve.wait_ge(xh_done, 2 * kt + 2)
                        nc.vector.tensor_tensor(XL[:, kt, :], banks[kt % 2][:], XH[:, kt, :].bitcast(f32), ALU.subtract).then_inc(xl_done, 1)
                        nc.vector.scalar_tensor_tensor(out=X16L[:, kt, :], in0=banks[kt % 2][:], scalar=X_SCALE, in1=X16H[:, kt, :],
                                                       op0=ALU.mult, op1=ALU.subtract).then_inc(xl_done, 1)
                    dve.wait_ge(ffn_loaded, 6 * 16)
                    dve.wait_ge(asum_done, 1)
                    for w in range(2):
                        link(nc.vector.tensor_reduce(asum[0:GRP, w:w + 1], GN[:, w].rearrange("p g j d -> p (g j d)"), AX.X, ALU.add,
                                                     apply_absolute_value=True))
                    nc.vector.tensor_reduce(asum[0:DO, 2:3], DN[0:DO].rearrange("p j d -> p (j d)"), AX.X, ALU.add,
                                            apply_absolute_value=True).then_inc(asum_done, 2)
                    for n in range(NWT):
                        og, kt = divmod(n, KT)
                        dve.wait_ge(wh_done, n + 1)
                        hi = WH[:, kt, og * D:(og + 1) * D] if og < 3 else OH[:, kt, :]
                        lo = WL[:, kt, og * D:(og + 1) * D] if og < 3 else OL[:, kt, :]
                        nc.vector.tensor_tensor(lo, banks[2 + n % RING][:], hi.bitcast(f32), ALU.subtract).then_inc(wl_done, 1)
                    dve.wait_ge(mean_ready, 1)
                    dve.wait_ge(evac_done, TILES)
                    link(nc.vector.tensor_scalar(mean[:], banks[0][:, 0:3], 1.0 / (OC * HO * DO), None, ALU.mult))
                    nc.vector.tensor_scalar(half[:], mean[:], 0.5, None, ALU.mult)
                    nc.vector.tensor_scalar(sig_scale[:], mean[:, 0:1], 1.0 / X_SCALE, None, ALU.mult)
                    link(nc.vector.tensor_tensor(gu_scale[:], mean[:, 0:1], mean[:, 1:2], ALU.mult))
                    link(nc.vector.tensor_scalar(ffn_scale[:], gu_scale[:], mean[:, 2:3], 1.0 / (X_SCALE * X_SCALE * H_SCALE), ALU.mult, ALU.mult))
                    link(nc.vector.tensor_scalar(nhalf[:], mean[:], -0.5, None, ALU.mult))
                    link(nc.vector.tensor_scalar(dneg, DN[:], nhalf[:, 2:3], None, ALU.is_lt))
                    nc.vector.scalar_tensor_tensor(out=dtern[:], in0=DN[:], scalar=half[:, 2:3], in1=dneg,
                                                   op0=ALU.is_gt, op1=ALU.subtract).then_inc(tern_dn, 1)
                    for w in range(2):
                        if w:
                            dve.wait_ge(tern_gu, w)
                        link(nc.vector.tensor_scalar(gneg, GN[:, w].rearrange("p g j d -> p (g j d)"), nhalf[0:GRP, w:w + 1], None, ALU.is_lt))
                        nc.vector.scalar_tensor_tensor(out=gtern[:, w].rearrange("p g j d -> p (g j d)"),
                                                       in0=GN[:, w].rearrange("p g j d -> p (g j d)"), scalar=half[0:GRP, w:w + 1], in1=gneg,
                                                       op0=ALU.is_gt, op1=ALU.subtract).then_inc(tern_gu, 1)
                    dve.wait_ge(tt_copied, NTT)
                    for k in range(OC):
                        for i in range(1, OC, 2):
                            j, sign = OCT[k][i]
                            last = nc.vector.tensor_scalar(MG[DO:P, i // 2, :, k * HO:(k + 1) * HO], TTs[DO:P, :, j, :], sign, None, ALU.mult)
                    last.then_inc(mg_done, 1)

            main = ExitStack()
            with main:
                HHs = alloc(main, "HHs", [P, HT, CH], f16)
                HLs = alloc(main, "HLs", [P, HT, CH], f16)
                qk_stage = [alloc(main, f"qk_stage{i}", [P, 3, CH], bf16) for i in range(2)]
                rest = [alloc(main, f"rest{i}", [P, CH], f32) for i in range(2)]
                v_stage = [alloc(main, f"v_stage{i}", [P, D], f32) for i in range(2)]
                g_stage = [alloc(main, f"g_stage{i}", [P, D], f32) for i in range(2)]
                sig = [alloc(main, f"sig{i}", [P, CH], f32) for i in range(2)]
                gated = [alloc(main, f"gated{i}", [P, CH], f32) for i in range(2)]
                hid = [alloc(main, f"hid{i}", [P, CH], f32) for i in range(2)]

                def bank_of(p):
                    return banks[2 + p % RING]

                def emptied(c, p):
                    if p >= RING:
                        return c * TILES + TILES + p - RING + 1
                    before = max(b for b in range(TILES) if b % RING == p % RING)
                    return c * TILES + before + 1

                def evacuated(c, p):
                    return c * TILES + TILES + p + 1

                block = main.enter_context(nc.Block())

                @block.sync
                def _(sp):
                    def chunk(c, more):
                        if more:
                            sp.wait_ge(xt_done, c * KT + KT)
                            sp.dma_start(xin[:], xf[bass.ds((c + 1) * CH, CH), :].rearrange("(t p) d -> p t d", p=P)).then_inc(x_loaded, 16)
                        for m in range(2 * KT):
                            scr = q_scr if m < KT else k_scr
                            sp.wait_ge(q3_done, c * 2 * KT + m + 1)
                            sp.dma_start(scr[bass.ds(c // 2, 1), :, (m % KT) * P:(m % KT + 1) * P, bass.ds(c % 2 * CH, CH)].rearrange("a r p t -> p (a r) t"),
                                         qk_stage[m % 2][:]).then_inc(qk_stored[m % 2], 16)
                        for t in range(TT):
                            sp.wait_ge(evac_done, evacuated(c, V0 + t))
                            sp.dma_start(v_scr[bass.ds(c * CH + t * P, P), :], v_stage[t % 2][:]).then_inc(v_stored[t % 2], 16)
                        for t in range(TT):
                            sp.wait_ge(evac_done, evacuated(c, DN0 + t))
                            sp.dma_start(g_scr[bass.ds(c * CH + t * P, P), :], g_stage[t % 2][:]).then_inc(g_stored[t % 2], 16)

                    with sp.Fori(0, NCH - 1) as c:
                        chunk(c, True)
                    chunk(NCH - 1, False)
                    for i in range(2):
                        sp.wait_ge(qk_stored[i], NCH * KT * 16)
                        sp.wait_ge(v_stored[i], NCH * TT // 2 * 16)
                        sp.wait_ge(g_stored[i], NCH * TT // 2 * 16)

                @block.gpsimd
                def _(pool):
                    def chunk(c):
                        for m in range(2 * KT):
                            pool.wait_ge(q2_done, c * 2 * KT + m + 1)
                            nc.gpsimd.tensor_tensor(qk_stage[m % 2][:, 2, :], rest[m % 2][:], qk_stage[m % 2][:, 1, :],
                                                    ALU.subtract).then_inc(q3_done, 1)
                        for t in range(HT):
                            n = hidden_rows(t)
                            pool.wait_ge(hh_done, c * HT + t + 1)
                            nc.gpsimd.tensor_tensor(HLs[0:n, t, :], hid[t % 2][0:n], HHs[0:n, t, :], ALU.subtract).then_inc(hl_done, 1)

                    with pool.Fori(0, NCH) as c:
                        chunk(c)

                @block.scalar
                def _(act):
                    def split(c, kt):
                        act.wait_ge(xt_done, c * KT + kt + 1)
                        nc.scalar.activation(XH[:, kt, :], banks[kt % 2][:], ACT.Identity).then_inc(xh_done, 1)
                        nc.scalar.activation(X16H[:, kt, :], banks[kt % 2][:], ACT.Identity, scale=X_SCALE).then_inc(xh_done, 1)

                    def high(c, t):
                        n = hidden_rows(t)
                        act.wait_ge(evac_done, evacuated(c, GU0 + 2 * t + 1))
                        nc.scalar.activation(HHs[0:n, t, :], hid[t % 2][0:n], ACT.Identity).then_inc(hh_done, 1)

                    def chunk(c, more):
                        for m in range(2 * KT):
                            act.wait_ge(tile_done, c * TILES + QK0 + m + 1)
                            act.wait_ge(qk_stored[m % 2], c * (KT * 16) + m // 2 * 16)
                            nc.scalar.activation(qk_stage[m % 2][:, 0, :], bank_of(QK0 + m)[:], ACT.Identity,
                                                 bias=bq_col[:, m:m + 1]).then_inc(q1_done, 1)
                        for t in range(HT):
                            p, n = GU0 + 2 * t, hidden_rows(t)
                            act.wait_ge(tile_done, c * TILES + p + 1)
                            if t >= 2:
                                act.wait_ge(evac_done, evacuated(c, p - 4))
                            nc.scalar.activation(sig[t % 2][0:n], bank_of(p)[0:n], ACT.Sigmoid, scale=sig_scale[0:n, 0:1]).then_inc(sig_done, 1)
                            if t >= 1:
                                high(c, t - 1)
                            if more and t == LN_AT[2] + 1:
                                root(act, c + 1)
                        high(c, HT - 1)
                        for t in range(TT):
                            if more and t < 2:
                                split(c + 1, 2 * t)
                                split(c + 1, 2 * t + 1)
                            p = DN0 + t
                            act.wait_ge(tile_done, c * TILES + p + 1)
                            if t >= 2:
                                act.wait_ge(evac_done, evacuated(c, p - 2))
                            nc.scalar.activation(sig[t % 2][:], bank_of(p)[:], ACT.Sigmoid, scale=ffn_scale[:, 0:1]).then_inc(sig_done, 1)

                    with act.Fori(0, NCH - 1) as c:
                        chunk(c, True)
                    chunk(NCH - 1, False)

                @block.vector
                def _(dve):
                    def split(c, kt):
                        dve.wait_ge(xh_done, c * 2 * KT + 2 * kt + 2)
                        nc.vector.tensor_tensor(XL[:, kt, :], banks[kt % 2][:], XH[:, kt, :].bitcast(f32), ALU.subtract).then_inc(xl_done, 1)
                        nc.vector.scalar_tensor_tensor(out=X16L[:, kt, :], in0=banks[kt % 2][:], scalar=X_SCALE, in1=X16H[:, kt, :],
                                                       op0=ALU.mult, op1=ALU.subtract).then_inc(xl_done, 1)

                    def chunk(c, more):
                        for m in range(2 * KT):
                            dve.wait_ge(q1_done, c * 2 * KT + m + 1)
                            nc.vector.scalar_tensor_tensor(out=rest[m % 2][:], in0=bank_of(QK0 + m)[:], scalar=bq_col[:, m:m + 1],
                                                           in1=qk_stage[m % 2][:, 0, :], op0=ALU.add, op1=ALU.subtract).then_inc(evac_done, 1)
                            dve.wait_ge(evac_done, evacuated(c, QK0 + m))
                            nc.vector.tensor_copy(qk_stage[m % 2][:, 1, :], rest[m % 2][:]).then_inc(q2_done, 1)
                        for t in range(TT):
                            dve.wait_ge(tile_done, c * TILES + V0 + t + 1)
                            dve.wait_ge(v_stored[t % 2], c * (TT // 2 * 16) + t // 2 * 16)
                            nc.vector.tensor_tensor(v_stage[t % 2][:].rearrange("p (q d h) -> p q h d", q=NQ, h=QH),
                                                    bank_of(V0 + t).rearrange("p (q h d) -> p q h d", q=NQ, h=QH),
                                                    bv_row[:].rearrange("p (q h d) -> p q h d", q=NQ, h=QH), ALU.add).then_inc(evac_done, 1)
                        for t in range(HT):
                            p, n = GU0 + 2 * t, hidden_rows(t)
                            dve.wait_ge(sig_done, c * (HT + TT) + t + 1)
                            nc.vector.tensor_tensor(gated[t % 2][0:n], bank_of(p)[0:n], sig[t % 2][0:n], ALU.mult).then_inc(evac_done, 1)
                            dve.wait_ge(tile_done, c * TILES + p + 2)
                            if more and t == LN_AT[1]:
                                dve.wait_ge(ln_step, (c + 1) * XLN + 4)
                            dve.wait_ge(evac_done, evacuated(c, p))
                            if t >= 2:
                                dve.wait_ge(hl_done, c * HT + t - 1)
                            nc.vector.scalar_tensor_tensor(out=hid[t % 2][0:n], in0=bank_of(p + 1)[0:n], scalar=H_SCALE,
                                                           in1=gated[t % 2][0:n], op0=ALU.mult, op1=ALU.mult).then_inc(evac_done, 1)
                            if more and t in LN_AT:
                                normalise(dve, c + 1, LN_AT.index(t))
                        for t in range(TT):
                            if more and t < 2:
                                split(c + 1, 2 * t)
                                split(c + 1, 2 * t + 1)
                            dve.wait_ge(sig_done, c * (HT + TT) + HT + t + 1)
                            dve.wait_ge(g_stored[t % 2], c * (TT // 2 * 16) + t // 2 * 16)
                            nc.vector.scalar_tensor_tensor(out=g_stage[t % 2][:], in0=bank_of(DN0 + t)[:], scalar=ffn_scale[:, 0:1],
                                                           in1=sig[t % 2][:], op0=ALU.mult, op1=ALU.mult).then_inc(evac_done, 1)

                    with dve.Fori(0, NCH - 1) as c:
                        chunk(c, True)
                    chunk(NCH - 1, False)

                @block.tensor
                def _(pe):
                    def transpose(c, kt):
                        if kt >= 2:
                            pe.wait_ge(xl_done, c * 2 * KT + 2 * (kt - 1))
                        for t in range(TT):
                            last = nc.tensor.transpose(banks[kt % 2][:, t * P:(t + 1) * P], xin[:, t, kt * P:(kt + 1) * P], identf[:])
                        last.then_inc(xt_done, 1)

                    def chunk(c, more):
                        pe.wait_ge(xl_done, c * 2 * KT + 2 * KT)
                        for m in range(2 * KT):
                            pe.wait_ge(evac_done, emptied(c, QK0 + m))
                            for kt in range(KT):
                                cols = slice(m * P, (m + 1) * P)
                                nc.tensor.matmul(bank_of(QK0 + m)[:], WH[:, kt, cols], XH[:, kt, :], start=(kt == 0), stop=False)
                                nc.tensor.matmul(bank_of(QK0 + m)[:], WH[:, kt, cols], XL[:, kt, :], start=False, stop=False)
                                last = nc.tensor.matmul(bank_of(QK0 + m)[:], WL[:, kt, cols], XH[:, kt, :], start=False, stop=(kt == KT - 1))
                            last.then_inc(tile_done, 1)
                        for t in range(TT):
                            pe.wait_ge(evac_done, emptied(c, V0 + t))
                            for kt in range(KT):
                                tok, cols = slice(t * P, (t + 1) * P), slice(2 * D, 3 * D)
                                nc.tensor.matmul(bank_of(V0 + t)[:], XH[:, kt, tok], WH[:, kt, cols], start=(kt == 0), stop=False)
                                nc.tensor.matmul(bank_of(V0 + t)[:], XH[:, kt, tok], WL[:, kt, cols], start=False, stop=False)
                                last = nc.tensor.matmul(bank_of(V0 + t)[:], XL[:, kt, tok], WH[:, kt, cols], start=False, stop=(kt == KT - 1))
                            last.then_inc(tile_done, 1)
                        for t in range(HT):
                            for w in range(2):
                                p, n = GU0 + 2 * t + w, hidden_rows(t)
                                pe.wait_ge(evac_done, emptied(c, p))
                                for kt in range(KT):
                                    wt = MG[:, kt, w, t * P:t * P + n]
                                    nc.tensor.matmul(bank_of(p)[0:n], wt, X16H[:, kt, :], start=(kt == 0), stop=False)
                                    last = nc.tensor.matmul(bank_of(p)[0:n], wt, X16L[:, kt, :], start=False, stop=(kt == KT - 1))
                                last.then_inc(tile_done, 1)
                        if more:
                            pe.wait_ge(ln_step, c * XLN + 2 * XLN)
                        for t in range(TT):
                            if more and t < 2:
                                transpose(c + 1, 2 * t)
                                transpose(c + 1, 2 * t + 1)
                            p, tok = DN0 + t, slice(t * P, (t + 1) * P)
                            pe.wait_ge(evac_done, emptied(c, p))
                            for k in range(HT):
                                n = hidden_rows(k)
                                if t == 0:
                                    pe.wait_ge(hl_done, c * HT + k + 1)
                                nc.tensor.matmul(bank_of(p)[:], HHs[0:n, k, tok], MD[0:n, k, :], start=(k == 0), stop=False)
                                last = nc.tensor.matmul(bank_of(p)[:], HLs[0:n, k, tok], MD[0:n, k, :], start=False, stop=(k == HT - 1))
                            last.then_inc(tile_done, 1)

                    pe.wait_ge(mg_done, 2)
                    pe.wait_ge(md_done, HT)
                    pe.wait_ge(wl_done, NWT)
                    with pe.Fori(0, NCH - 1) as c:
                        chunk(c, True)
                    chunk(NCH - 1, False)

        two = ExitStack()
        with two:
            Qs = [alloc(two, f"Qs{i}", [P, QH, S], bf16) for i in range(SLOTS)]
            Ks = [alloc(two, f"Ks{i}", [P, QH, S], bf16) for i in range(SLOTS)]
            Vs = [alloc(two, f"Vs{i}", [P, KB, 2 * QH * HD], f32) for i in range(SLOTS)]
            probs = [alloc(two, f"probs{i}", [P, QH, CH], f32) for i in range(PSLOTS)]
            mx = [alloc(two, f"mx{i}", [P, QH, KB], f32) for i in range(2)]
            mx2 = [alloc(two, f"mx2{i}", [P, QH, KB // 2], f32) for i in range(2)]
            mrest = alloc(two, "mrest", [P, QH * KB], f32)
            mparts = alloc(two, "mparts", [P, 3, QH * KB], bf16)
            mrows = alloc(two, "mrows", [3 * QH * KB, P], bf16)
            osum = [alloc(two, f"osum{i}", [P, CH], f32) for i in range(2)]

            fixed = sem("fixed")
            stacked = [sem(f"stacked{i}") for i in range(SLOTS)]
            max_filled = sem("max_filled")
            max_read = sem("max_read")
            max_step = sem("max_step")
            mt_filled = sem("mt_filled")
            mt_copied = sem("mt_copied")
            m_stacked = sem("m_stacked")
            s_filled = sem("s_filled")
            exp_done = sem("exp_done")
            pv_done = sem("pv_done")
            o_copied = sem("o_copied")
            o_stored = [sem(f"o_stored{i}") for i in range(2)]

            NLOAD = 2 * len(TERM_Q) + 2
            MSTEP = 5
            s_bank = [psum[:, 0:2, :], psum[:, 2:4, :]]
            m_bank = [banks[4], banks[5]]
            pv_bank, mt_bank = banks[6], banks[7]

            def stack_uses(t, s):
                return ((t - s) // SLOTS + 1) * NLOAD * 16

            block = two.enter_context(nc.Block())

            @block.sync
            def _(sp):
                def load(t, s, free):
                    if free:
                        sp.wait_ge(pv_done, (t - SLOTS) * NST + NST + PSLOTS)
                    b, hq = t // NQ, t % NQ
                    for n, (qp, kp) in enumerate(zip(TERM_Q, TERM_K)):
                        rows = slice(n * HD, (n + 1) * HD)
                        for dst, scr, part in ((Qs, q_scr, qp), (Ks, k_scr, kp)):
                            sp.dma_start(dst[s][rows], scr[bass.ds(b, 1), part, bass.ds(hq * (QH * HD), QH * HD)].rearrange("a (h d) t -> d (a h) t", d=HD)
                                         ).then_inc(stacked[s], 16)
                    sp.dma_start(Ks[s][ROWS_QK:ROWS_MAX], alibi[bass.ds(hq * QH, QH)].rearrange("h r t -> r h t")).then_inc(stacked[s], 16)
                    sp.dma_start(Vs[s][:, :, 0:QH * HD], v_scr[bass.ds(b * S, S), bass.ds(hq * (QH * HD), QH * HD)].rearrange("(k p) c -> p k c", p=P)
                                 ).then_inc(stacked[s], 16)

                def maximum(t, s):
                    sp.wait_ge(mt_copied, t + 1)
                    sp.dma_start(Qs[s][ROWS_MAX:ROWS_ALL], mrows[:]).then_inc(m_stacked, 16)

                def store(t, c):
                    sp.wait_ge(o_copied, t * 2 + c + 1)
                    sp.dma_start(o_scr[bass.ds(t // NQ, 1), c, bass.ds(t % NQ, 1)].rearrange("a b p t -> p (a b) t"), osum[c][:]
                                 ).then_inc(o_stored[c], 16)

                def step(t, s, ahead, lead):
                    if lead:
                        load(t + 2, (s + 2) % SLOTS, True)
                    store(t, 0)
                    if ahead:
                        maximum(t + 1, (s + 1) % SLOTS)
                    store(t, 1)

                sp.wait_ge(fixed, 3 * SLOTS)
                load(0, 0, False)
                load(1, 1, False)
                maximum(0, 0)
                load(2, 2, False)
                store(0, 0)
                maximum(1, 1)
                store(0, 1)
                with sp.Fori(0, 4) as g:
                    for s in range(SLOTS):
                        step(g * SLOTS + s + 1, (s + 1) % SLOTS, True, True)
                step(13, 1, True, True)
                step(14, 2, True, False)
                step(15, 0, False, False)
                for c in range(2):
                    sp.wait_ge(o_stored[c], QUADS * 16)

            @block.gpsimd
            def _(pool):
                for i in range(SLOTS):
                    nc.gpsimd.memset(Vs[i][:, :, QH * HD:], 1.0).then_inc(fixed, 1)
                nc.gpsimd.memset(mx2[0][:], 0.0).then_inc(exp_done, 2)
                nc.gpsimd.memset(mx2[1][:], 0.0).then_inc(max_read, 2)
                nc.gpsimd.memset(mrest[:], 0.0).then_inc(pv_done, PSLOTS)
                pool.wait_ge(pv_done, PSLOTS)
                for i in range(SLOTS):
                    nc.gpsimd.memset(Qs[i][ROWS_QK:P], 1.0).then_inc(fixed, 1)
                    nc.gpsimd.memset(Ks[i][ROWS_QK:P], 1.0).then_inc(fixed, 1)

            @block.scalar
            def _(act):
                def step(t):
                    for n, (c, kb) in enumerate(STEPS):
                        cols = CH - P * max(0, kb - 4 * c)
                        for pair in range(2):
                            u = 2 * n + pair
                            act.wait_ge(s_filled, t * (2 * NST) + u + 1)
                            act.wait_ge(pv_done, t * NST + n + 1)
                            nc.scalar.activation(probs[n % PSLOTS][:, 2 * pair:2 * pair + 2, 0:cols], s_bank[pair][:, :, 0:cols],
                                                 ACT.Exp, scale=1.0 / INV_SCALE).then_inc(exp_done, 1)
                        if n == 4 + LAG - 1:
                            copy_out(t, 0)
                    copy_out(t, 1)

                def copy_out(t, c):
                    n = 3 if c == 0 else NST - 1
                    act.wait_ge(pv_done, t * NST + n + 1 + PSLOTS)
                    act.wait_ge(o_stored[c], t * 16)
                    nc.scalar.activation(osum[c][:], pv_bank[:], ACT.Copy).then_inc(o_copied, 1)

                with act.Fori(0, QUADS) as t:
                    step(t)

            @block.vector
            def _(dve):
                def read_max(t, j, s):
                    qb, h, n, k0, keys = MAXT[j]
                    dve.wait_ge(max_filled, t * NMAX + j + 1)
                    dst = mx[s][:, h:h + n, qb:qb + 1] if k0 == 0 else mx2[s][:, h:h + n, qb - 4:qb - 3]
                    nc.vector.tensor_reduce(dst, m_bank[j % 2][:, 0:n * keys].rearrange("p (n k) -> p n k", n=n), AX.X, ALU.max
                                            ).then_inc(max_read, 1)

                def parts(t, s):
                    dve.wait_ge(max_read, t * NMAX + NMAX + 2)
                    nc.vector.tensor_tensor(mx[s][:, :, 4:8], mx[s][:, :, 4:8], mx2[s][:], ALU.max).then_inc(max_step, 1)
                    flat = mx[s][:].rearrange("p h q -> p (h q)")
                    dve.wait_ge(max_step, t * MSTEP + 1)
                    dve.wait_ge(mt_filled, t)
                    nc.vector.tensor_scalar(mparts[:, 0, :], flat, -1.0, None, ALU.mult).then_inc(max_step, 1)
                    dve.wait_ge(max_step, t * MSTEP + 2)
                    nc.vector.scalar_tensor_tensor(out=mrest[:], in0=flat, scalar=-1.0, in1=mparts[:, 0, :], op0=ALU.mult,
                                                   op1=ALU.subtract).then_inc(max_step, 1)
                    dve.wait_ge(max_step, t * MSTEP + 3)
                    nc.vector.tensor_copy(mparts[:, 1, :], mrest[:]).then_inc(max_step, 1)
                    dve.wait_ge(max_step, t * MSTEP + 4)
                    nc.vector.tensor_tensor(mparts[:, 2, :], mrest[:], mparts[:, 1, :], ALU.subtract).then_inc(max_step, 1)

                def rows(t):
                    dve.wait_ge(mt_filled, t + 1)
                    dve.wait_ge(m_stacked, t * 16)
                    nc.vector.tensor_copy(mrows[:], mt_bank[0:3 * QH * KB, 0:P // 2].bitcast(bf16)).then_inc(mt_copied, 1)

                dve.wait_ge(max_read, 2)
                dve.wait_ge(exp_done, 2)
                dve.wait_ge(pv_done, PSLOTS)
                with dve.Fori(0, QUADS // 2) as g:
                    for s in range(2):
                        t = g * 2 + s
                        for j in range(NMAX):
                            read_max(t, j, s)
                        parts(t, s)
                        rows(t)

            @block.tensor
            def _(pe):
                def fill_max(t, j, s):
                    qb, h, n, k0, keys = MAXT[j]
                    if j == 0:
                        pe.wait_ge(stacked[s], stack_uses(t, s))
                    pe.wait_ge(max_read, t * NMAX + j + 1)
                    masked = k0 + keys == (qb + 1) * P
                    for i in range(n):
                        dst = m_bank[j % 2][:, i * keys:(i + 1) * keys]
                        last = nc.tensor.matmul(dst, Qs[s][0:ROWS_MAX, h + i, qb * P:(qb + 1) * P], Ks[s][0:ROWS_MAX, h + i, k0:k0 + keys],
                                                start=True, stop=not masked)
                        if masked:
                            last = nc.tensor.matmul(dst[:, keys - P:keys], identb[:], causal[:], start=False, stop=True)
                    last.then_inc(max_filled, 1)

                def transpose_max(t):
                    pe.wait_ge(max_step, t * MSTEP + MSTEP)
                    nc.tensor.transpose(mt_bank[0:3 * QH * KB, 0:P // 2].bitcast(bf16), mparts[:].rearrange("p r n -> p (r n)"), identb[:]
                                        ).then_inc(mt_filled, 1)

                def scores(t, n, s):
                    c, kb = STEPS[n]
                    q0 = P * max(0, kb - 4 * c)
                    for pair in range(2):
                        pe.wait_ge(exp_done, t * (2 * NST) + 2 * n + pair + 1)
                        for h in range(2):
                            last = nc.tensor.matmul(s_bank[pair][:, h, 0:CH - q0], Ks[s][0:ROWS_ALL, 2 * pair + h, kb * P:(kb + 1) * P],
                                                    Qs[s][0:ROWS_ALL, 2 * pair + h, c * CH + q0:(c + 1) * CH], start=True, stop=not DIAG[n])
                            if DIAG[n]:
                                last = nc.tensor.matmul(s_bank[pair][:, h, 0:P], causal[:], identb[:], start=False, stop=True)
                        last.then_inc(s_filled, 1)

                def products(t, n, s):
                    c, kb = STEPS[n]
                    q0 = P * max(0, kb - 4 * c)
                    pe.wait_ge(exp_done, t * (2 * NST) + 2 * n + 2 + 2)
                    if kb == 0:
                        pe.wait_ge(o_copied, t * 2 + c)
                    for h in range(QH):
                        last = nc.tensor.matmul(pv_bank[32 * h:32 * h + 32, q0:CH], Vs[s][:, kb, h::QH],
                                                probs[n % PSLOTS][:, h, 0:CH - q0], start=(kb == 0), stop=(kb == 4 * c + 3))
                    last.then_inc(pv_done, 1)

                def step(t, s, ahead, lead):
                    todo = ([(1, j) for j in range(LEAD, NMAX)] if ahead else []) + ([(2, j) for j in range(LEAD)] if lead else [])
                    total = len(todo)
                    pe.wait_ge(m_stacked, t * 16 + 16)
                    transposed = False
                    for n in range(NST + LAG):
                        if n < NST:
                            scores(t, n, s)
                        upto = total * (n + 1) // (NST + LAG)
                        while total - len(todo) < upto:
                            a, j = todo.pop(0)
                            fill_max(t + a, j, (s + a) % SLOTS)
                            if ahead and not transposed and (a == 2 and j == 1 or not todo):
                                transpose_max(t + 1)
                                transposed = True
                        if n >= LAG:
                            products(t, n - LAG, s)

                pe.wait_ge(fixed, 3 * SLOTS)
                for j in range(NMAX):
                    fill_max(0, j, 0)
                transpose_max(0)
                for j in range(LEAD):
                    fill_max(1, j, 1)
                step(0, 0, True, True)
                with pe.Fori(0, 4) as g:
                    for s in range(SLOTS):
                        step(g * SLOTS + s + 1, (s + 1) % SLOTS, True, True)
                step(13, 1, True, True)
                step(14, 2, True, False)
                step(15, 0, False, False)

        three = ExitStack()
        with three:
            den = alloc(three, "den", [P, KT, CH], f32)
            num = alloc(three, "num", [P, KT, CH], f32)
            AH = alloc(three, "AH", [P, KT, CH], f32r)
            AL = alloc(three, "AL", [P, KT, CH], f32r)
            gate = alloc(three, "gate", [P, TT, D], f32)
            xres = alloc(three, "xres", [P, TT, D], f32)
            scaled = [alloc(three, f"scaled{i}", [P, D], f32) for i in range(2)]
            fin = [alloc(three, f"fin{i}", [P, D], f32) for i in range(2)]

            sums_loaded = sem("sums_loaded")
            tok_loaded = sem("tok_loaded")
            rec_done = sem("rec_done")
            att_done = sem("att_done")
            ah_done = sem("ah_done")
            al_done = sem("al_done")
            proj_done = sem("proj_done")
            proj_read = sem("proj_read")
            gated_done = sem("gated_done")
            fin_done = sem("fin_done")
            fin_stored = [sem(f"fin_stored{i}") for i in range(2)]

            block = three.enter_context(nc.Block())

            @block.sync
            def _(sp):
                with sp.Fori(0, NCH) as c:
                    sp.wait_ge(att_done, c * KT)
                    for x_, dst in enumerate((num, den)):
                        for u in range(2):
                            for kt in range(KT):
                                src = o_scr[bass.ds(c // 2, 1), bass.ds(c % 2, 1), 2 * kt + u].rearrange("a b (h x d) t -> x (a b h) d t", x=2, d=HD)
                                sp.dma_start(dst[QH * HD * u:QH * HD * (u + 1), kt], src[x_]).then_inc(sums_loaded, 16)
                    sp.wait_ge(fin_done, c * TT)
                    sp.dma_start(gate[:], g_scr[bass.ds(c * CH, CH), :].rearrange("(t p) d -> p t d", p=P)).then_inc(tok_loaded, 16)
                    sp.dma_start(xres[:], xf[bass.ds(c * CH, CH), :].rearrange("(t p) d -> p t d", p=P)).then_inc(tok_loaded, 16)
                    for t in range(TT):
                        sp.wait_ge(fin_done, c * TT + t + 1)
                        sp.dma_start(outf[bass.ds(c * CH + t * P, P), :], fin[t % 2][:]).then_inc(fin_stored[t % 2], 16)
                for i in range(2):
                    sp.wait_ge(fin_stored[i], NCH * TT // 2 * 16)

            @block.vector
            def _(dve):
                with dve.Fori(0, NCH) as c:
                    dve.wait_ge(sums_loaded, c * (4 * KT * 16) + 4 * KT * 16)
                    for kt in range(KT):
                        nc.vector.reciprocal(den[:, kt, :], den[:, kt, :]).then_inc(rec_done, 1)
                    for kt in range(KT):
                        dve.wait_ge(rec_done, c * KT + kt + 1)
                        nc.vector.tensor_tensor(num[:, kt, :], num[:, kt, :], den[:, kt, :], ALU.mult).then_inc(att_done, 1)
                    for kt in range(KT):
                        dve.wait_ge(ah_done, c * KT + kt + 1)
                        nc.vector.tensor_tensor(AL[:, kt, :], num[:, kt, :], AH[:, kt, :].bitcast(f32), ALU.subtract).then_inc(al_done, 1)
                    dve.wait_ge(tok_loaded, c * 32 + 32)
                    for t in range(TT):
                        dve.wait_ge(proj_done, c * TT + t + 1)
                        nc.vector.tensor_tensor(scaled[t % 2][:], banks[t][:], bo_row[:], ALU.add).then_inc(proj_read, 1)
                        dve.wait_ge(proj_read, c * TT + t + 1)
                        nc.vector.tensor_tensor(scaled[t % 2][:], scaled[t % 2][:], gate[:, t, :], ALU.mult).then_inc(gated_done, 1)
                        dve.wait_ge(gated_done, c * TT + t + 1)
                        dve.wait_ge(fin_stored[t % 2], c * (TT // 2 * 16) + t // 2 * 16)
                        nc.vector.tensor_tensor(fin[t % 2][:], scaled[t % 2][:], xres[:, t, :], ALU.add).then_inc(fin_done, 1)

            @block.scalar
            def _(act):
                with act.Fori(0, NCH) as c:
                    for kt in range(KT):
                        act.wait_ge(att_done, c * KT + kt + 1)
                        act.wait_ge(proj_done, c * TT)
                        nc.scalar.activation(AH[:, kt, :], num[:, kt, :], ACT.Copy).then_inc(ah_done, 1)

            @block.tensor
            def _(pe):
                with pe.Fori(0, NCH) as c:
                    pe.wait_ge(al_done, c * KT + KT)
                    for t in range(TT):
                        tok = slice(t * P, (t + 1) * P)
                        pe.wait_ge(proj_read, c * TT)
                        for kt in range(KT):
                            nc.tensor.matmul(banks[t][:], AH[:, kt, tok], OH[:, kt, :], start=(kt == 0), stop=False)
                            nc.tensor.matmul(banks[t][:], AH[:, kt, tok], OL[:, kt, :], start=False, stop=False)
                            last = nc.tensor.matmul(banks[t][:], AL[:, kt, tok], OH[:, kt, :], start=False, stop=(kt == KT - 1))
                        last.then_inc(proj_done, 1)


def alibi_parts():
    import numpy as np

    m = np.arange(1, H + 1, dtype=np.float32) * np.float32(8 / H)
    slopes = np.float32(1.0) / np.power(np.float32(2.0), m)
    rest = slopes[:, None] * np.arange(1 - S, 1, dtype=np.float32)[None, :] * np.float32(INV_SCALE)
    parts = []
    for _ in range(3):
        bits = rest.view(np.uint32) & np.uint32(0xFFFF0000)
        parts.append((bits >> 16).astype(np.uint16))
        rest = rest - bits.view(np.float32)
    return np.ascontiguousarray(np.stack(parts, axis=1))


_INS = ["L0_attn_x", "L0_attn_w_qkv", "L0_attn_b_qkv", "L0_attn_w_out", "L0_attn_b_out", "L0_ffn_w_gate", "L0_ffn_w_up", "L0_ffn_w_down"]


def kernel(**inputs):
    import numpy as np
    import concourse.bacc as bacc
    from concourse.bass_utils import run_bass_kernel_spmd

    nc = bacc.Bacc("TRN2", target_bir_lowering=False, num_devices=1)
    arrays = {f"in_{name}": np.ascontiguousarray(inputs[name]) for name in _INS}
    args = [nc.dram_tensor(n, a.shape, mybir.dt.from_np(a.dtype), kind="ExternalInput").ap() for n, a in arrays.items()]
    arrays["alibi"] = alibi_parts()
    alibi = nc.dram_tensor("alibi", arrays["alibi"].shape, mybir.dt.uint16, kind="ExternalInput").ap().bitcast(mybir.dt.bfloat16)
    out = nc.dram_tensor("out", (B, S, D), mybir.dt.float32, kind="ExternalOutput").ap()
    program(nc, *args, alibi, out)
    r = run_bass_kernel_spmd(nc, [arrays], core_ids=[0])
    return r.results[0]["out"]
```

```python
import concourse.bass as bass
from concourse import mybir
from contextlib import ExitStack

B, S, D, H = 2, 1024, 512, 32
HD = D // H
T = B * S
P = 128
KT = D // P
CH = 512
NCH = T // CH
TT = CH // P
OC = 8
HO, DO = 1366 // OC, D // OC
HID = OC * HO
HT = -(-HID // P)
GRP = HO // 2
EPS = 1e-5
TRIPLES = [(1, 2, 3), (1, 4, 5), (1, 7, 6), (2, 4, 6), (2, 5, 7), (3, 4, 7), (3, 6, 5)]

QH = 4
NQ = H // QH
QUADS = B * NQ
KB = S // P
TERM_Q = [0, 0, 1, 1, 0, 2]
TERM_K = [0, 1, 0, 1, 2, 0]
ROWS_QK = HD * len(TERM_Q)
ROWS_MAX = ROWS_QK + 3
ROWS_ALL = ROWS_MAX + 3
SLOTS = 3
INV_SCALE = 4.0
MASKED = -1.0e9 * INV_SCALE

X_SCALE = 256.0
H_SCALE = 2.0 ** -19


def octonion():
    by = [[None] * OC for _ in range(OC)]
    by[0][0] = (0, 1.0)
    for i in range(1, OC):
        by[i][i] = (0, 1.0)
        by[i][0] = (i, 1.0)
        by[0][i] = (i, -1.0)
    for a, b, c in TRIPLES:
        for x, y, z in ((a, b, c), (b, c, a), (c, a, b)):
            by[z][y] = (x, 1.0)
            by[z][x] = (y, -1.0)
    return by


OCT = octonion()

QK0, V0, GU0, DN0 = 0, 2 * KT, 2 * KT + TT, 2 * KT + TT + 2 * HT
TILES = DN0 + TT
LAST = NCH - 1
LN_AT = [1, 2, 3, 6, 7]
LN_STEPS = 4 + 4 + 1 + 4 + 4
NSIG = 3


def hidden_rows(t):
    return min(P, HID - t * P)


def max_tiles():
    out = []
    for half in range(2):
        for qb in range(4 * half, KB):
            keys = min(CH, P * (qb + 1) - CH * half)
            n = CH // keys
            for h in range(0, QH, n):
                out.append((qb, h, min(n, QH - h), CH * half, keys))
    return out


MAXT = max_tiles()
NMAX = len(MAXT)
STEPS = [(c, kb) for c in range(S // CH) for kb in range(4 * (c + 1))]
NST = len(STEPS)
COLS = [CH - P * max(0, kb - 4 * c) for c, kb in STEPS]
DIAG = [kb >= 4 * c for c, kb in STEPS]
LEAD = 10
LAG = 2
PSLOTS = 4


def interleave(ahead, lead):
    main = []
    for n in range(NST + LAG):
        if n < NST:
            main += [("scores", n, pair, 2 * COLS[n] + 2 * P * DIAG[n]) for pair in range(2)]
        if n >= LAG:
            main.append(("products", n - LAG, 0, 4 * COLS[n - LAG]))
    tiles = ([(1, j) for j in range(LEAD, NMAX)] if ahead else []) + ([(2, j) for j in range(LEAD)] if lead else [])
    cost = [MAXT[j][2] * MAXT[j][4] + 64 for _, j in tiles]
    whole, done, out, spent = sum(m[3] for m in main), 0, [], 0
    for m in main:
        out.append(m[:3])
        done += m[3]
        while tiles and (spent + cost[0] / 2) * whole <= done * (sum(cost) + spent):
            spent += cost.pop(0)
            out.append(("maximum", *tiles.pop(0)))
    return out + [("maximum", *x) for x in tiles]


def program(nc, x, w_qkv, b_qkv, w_out, b_out, w_gate, w_up, w_down, alibi, out):
    f32, f32r, bf16, f16 = mybir.dt.float32, mybir.dt.float32r, mybir.dt.bfloat16, mybir.dt.float16
    ALU, ACT, AX = mybir.AluOpType, mybir.ActivationFunctionType, mybir.AxisListType

    q_scr = nc.dram_tensor("q_scr", [B, 3, D, S], bf16, kind="Internal").ap()
    k_scr = nc.dram_tensor("k_scr", [B, 3, D, S], bf16, kind="Internal").ap()
    v_scr = nc.dram_tensor("v_scr", [T, D], f32, kind="Internal").ap()
    g_scr = nc.dram_tensor("g_scr", [T, D], f32, kind="Internal").ap()
    o_scr = nc.dram_tensor("o_scr", [B, 2, NQ, P, CH], f32, kind="Internal").ap()
    r_scr = nc.dram_tensor("r_scr", [B, 2, NQ, QH, CH], f32, kind="Internal").ap()

    xf = x.rearrange("b s d -> (b s) d")
    outf = out.rearrange("b s d -> (b s) d")

    top = ExitStack()
    with top:
        def alloc(stack, name, shape, dt):
            return stack.enter_context(nc.sbuf_tensor(name, shape, dt))

        def sem(name):
            return top.enter_context(nc.semaphore(name))

        psum = top.enter_context(nc.psum_tensor("psum", [P, 8, CH], f32))
        banks = [psum[:, i, :] for i in range(8)]
        identf = alloc(top, "identf", [P, P], f32)
        identb = alloc(top, "identb", [P, P], bf16)
        causal = alloc(top, "causal", [P, P], bf16)
        ones = alloc(top, "ones", [P, P], f32)
        primer = alloc(top, "primer", [P, 16], f32)
        OH = alloc(top, "OH", [P, KT, D], f32r)
        OL = alloc(top, "OL", [P, KT, D], f32r)

        ffn = ExitStack()
        top.enter_context(ffn)
        MG = alloc(ffn, "MG", [P, KT, 2, HID], f16)
        MD = alloc(ffn, "MD", [P, HT, D], f16)
        X16H = alloc(ffn, "X16H", [P, KT, CH], f16)
        X16L = alloc(ffn, "X16L", [P, KT, CH], f16)
        shared = alloc(ffn, "shared", [P, HT * CH], f32)
        HHs = shared[:, 0:HT * CH // 2].bitcast(f16).rearrange("p (t n) -> p t n", t=HT)
        HLs = shared[:, HT * CH // 2:].bitcast(f16).rearrange("p (t n) -> p t n", t=HT)
        NG, ND = 2 * 2 * OC * DO, OC * HO
        GN = shared[0:GRP, 0:NG].rearrange("p (w g j d) -> p w g j d", w=2, g=2, j=OC)
        DN = shared[:, NG:NG + ND].rearrange("p (j d) -> p j d", j=OC)
        gtern = shared[0:GRP, NG + ND:NG + ND + NG // 2].bitcast(bf16).rearrange("p (w g j d) -> p w g j d", w=2, g=2, j=OC)
        dtern = shared[:, NG + ND + NG // 2:NG + ND + NG // 2 + ND // 2].bitcast(bf16).rearrange("p (j d) -> p j d", j=OC)
        hid = [alloc(ffn, f"hid{i}", [P, CH], f32) for i in range(NSIG)]
        g_stage = [alloc(ffn, f"g_stage{i}", [P, D], f32) for i in range(2)]
        sig_scale = alloc(ffn, "sig_scale", [P, 1], f32)
        ffn_scale = alloc(ffn, "ffn_scale", [P, 1], f32)

        s_const = sem("s_const")
        x_loaded = sem("x_loaded")
        w_loaded = [sem(f"w_loaded{i}") for i in range(2)]
        ffn_loaded = sem("ffn_loaded")
        bias_loaded = sem("bias_loaded")
        ln_step = sem("ln_step")
        std_done = sem("std_done")
        xt_done = sem("xt_done")
        xh_done = sem("xh_done")
        xl_done = sem("xl_done")
        wt_done = sem("wt_done")
        wh_done = sem("wh_done")
        wl_done = sem("wl_done")
        dve_prep = sem("dve_prep")
        asum_done = sem("asum_done")
        mean_ready = sem("mean_ready")
        tern_gu = sem("tern_gu")
        tern_dn = sem("tern_dn")
        tt_done = sem("tt_done")
        tt_copied = sem("tt_copied")
        mg_done = sem("mg_done")
        mdn_done = sem("mdn_done")
        mdt_done = sem("mdt_done")
        md_done = sem("md_done")
        tile_done = sem("tile_done")
        evac_done = sem("evac_done")
        q1_done = sem("q1_done")
        q2_done = sem("q2_done")
        q3_done = sem("q3_done")
        sig_done = sem("sig_done")
        hh_done = sem("hh_done")
        hl_done = sem("hl_done")
        qk_stored = [sem(f"qk_stored{i}") for i in range(2)]
        v_stored = [sem(f"v_stored{i}") for i in range(2)]
        g_stored = [sem(f"g_stored{i}") for i in range(2)]

        def evacuated(c, p):
            return c * TILES + TILES + p + 1

        def pe_gated(pe, c, bank, free, beside):
            for t in range(HT):
                for w in range(2):
                    p, n = GU0 + 2 * t + w, hidden_rows(t)
                    free(c, p)
                    for kt in range(KT):
                        wt = MG[:, kt, w, t * P:t * P + n]
                        nc.tensor.matmul(bank(p)[0:n], wt, X16H[:, kt, :], start=(kt == 0), stop=False)
                        last = nc.tensor.matmul(bank(p)[0:n], wt, X16L[:, kt, :], start=False, stop=(kt == KT - 1))
                    last.then_inc(tile_done, 1)
                    beside(p)
            for t in range(TT):
                p, tok = DN0 + t, slice(t * P, (t + 1) * P)
                free(c, p)
                for k in range(HT):
                    n = hidden_rows(k)
                    if t == 0:
                        pe.wait_ge(hl_done, c * HT + k + 1)
                    nc.tensor.matmul(bank(p), HHs[0:n, k, tok], MD[0:n, k, :], start=(k == 0), stop=False)
                    last = nc.tensor.matmul(bank(p), HLs[0:n, k, tok], MD[0:n, k, :], start=False, stop=(k == HT - 1))
                last.then_inc(tile_done, 1)
                beside(p)

        def act_gated(act, c, bank, beside):
            def high(t):
                n = hidden_rows(t)
                act.wait_ge(evac_done, evacuated(c, GU0 + 2 * t + 1))
                nc.scalar.activation(HHs[0:n, t, :], hid[t % NSIG][0:n], ACT.Identity).then_inc(hh_done, 1)

            for t in range(HT):
                p, n = GU0 + 2 * t, hidden_rows(t)
                act.wait_ge(tile_done, c * TILES + p + 1)
                if t >= NSIG:
                    act.wait_ge(hl_done, c * HT + t - NSIG + 1)
                nc.scalar.activation(hid[t % NSIG][0:n], bank(p)[0:n], ACT.Sigmoid, scale=sig_scale[0:n, 0:1]).then_inc(sig_done, 1)
                if t >= 1:
                    high(t - 1)
                beside(p)
            high(HT - 1)
            for t in range(TT):
                p = DN0 + t
                act.wait_ge(tile_done, c * TILES + p + 1)
                if t >= NSIG:
                    act.wait_ge(evac_done, evacuated(c, p - NSIG))
                nc.scalar.activation(hid[(HT + t) % NSIG][:], bank(p), ACT.Sigmoid, scale=ffn_scale[:, 0:1]).then_inc(sig_done, 1)
                beside(p)

        def dve_gated(dve, c, bank, beside):
            for t in range(HT):
                p, n, h = GU0 + 2 * t, hidden_rows(t), hid[t % NSIG]
                dve.wait_ge(sig_done, c * (HT + TT) + t + 1)
                nc.vector.tensor_tensor(h[0:n], bank(p)[0:n], h[0:n], ALU.mult).then_inc(evac_done, 1)
                beside(p)
                dve.wait_ge(tile_done, c * TILES + p + 2)
                dve.wait_ge(evac_done, evacuated(c, p))
                nc.vector.scalar_tensor_tensor(out=h[0:n], in0=bank(p + 1)[0:n], scalar=H_SCALE, in1=h[0:n],
                                               op0=ALU.mult, op1=ALU.mult).then_inc(evac_done, 1)
                beside(p + 1)
            for t in range(TT):
                dve.wait_ge(sig_done, c * (HT + TT) + HT + t + 1)
                dve.wait_ge(g_stored[t % 2], c * (TT // 2 * 16) + t // 2 * 16 + 16)
                nc.vector.scalar_tensor_tensor(out=g_stage[t % 2][:], in0=bank(DN0 + t), scalar=ffn_scale[:, 0:1],
                                               in1=hid[(HT + t) % NSIG][:], op0=ALU.mult, op1=ALU.mult).then_inc(evac_done, 1)
                beside(DN0 + t)

        def pool_gated(pool, c):
            for t in range(HT):
                n = hidden_rows(t)
                pool.wait_ge(hh_done, c * HT + t + 1)
                nc.gpsimd.tensor_tensor(HLs[0:n, t, :], hid[t % NSIG][0:n], HHs[0:n, t, :], ALU.subtract).then_inc(hl_done, 1)

        def sp_gated(sp, c):
            for t in range(TT):
                sp.wait_ge(evac_done, evacuated(c, DN0 + t))
                sp.dma_start(g_scr[bass.ds(c * CH + t * P, P), :], g_stage[t % 2][:]).then_inc(g_stored[t % 2], 16)

        one = ExitStack()
        with one:
            WH = alloc(one, "WH", [P, KT, 3 * D], f32r)
            WL = alloc(one, "WL", [P, KT, 3 * D], f32r)
            XH = alloc(one, "XH", [P, KT, CH], f32r)
            XL = alloc(one, "XL", [P, KT, CH], f32r)
            xin = alloc(one, "xin", [P, TT, D], f32)
            wnat = alloc(one, "wnat", [P, 2 * KT * D], f32)
            wslot = [wnat[:, i * KT * D:(i + 1) * KT * D].rearrange("p (t d) -> p t d", t=KT) for i in range(2)]
            NMDN = OC // 2 * ND
            MDn = wnat[:, 0:NMDN // 2].bitcast(bf16).rearrange("p (k i d) -> p k i d", k=OC // 2, i=OC)
            TTs = wnat[:, NMDN // 2:NMDN // 2 + ND].bitcast(bf16).rearrange("p (w j o) -> p w j o", w=2, j=OC)
            dneg = TTs[:, 0]
            gneg = TTs[0:GRP, 1].rearrange("p j o -> p (j o)")[:, 0:NG // 2]
            qk_stage = [alloc(one, f"qk_stage{i}", [P, 3, CH], bf16) for i in range(2)]
            rest = [alloc(one, f"rest{i}", [P, CH], f32) for i in range(2)]
            v_stage = [alloc(one, f"v_stage{i}", [P, D], f32) for i in range(2)]
            stats = alloc(one, "stats", [P, TT, 6], f32)
            moments = alloc(one, "moments", [P, TT, 2], f32)
            var_eps = alloc(one, "var_eps", [P, TT], f32)
            std = alloc(one, "std", [P, TT], f32)
            rstd0 = alloc(one, "rstd0", [P, TT], f32)
            rstd = alloc(one, "rstd", [P, TT], f32)
            newton = alloc(one, "newton", [P, 2, TT], f32)
            bq_col = alloc(one, "bq_col", [P, 2 * KT], f32)
            bv_row = alloc(one, "bv_row", [P, D], f32)
            asum = alloc(one, "asum", [P, 3], f32)
            mean = alloc(one, "mean", [P, 3], f32)
            half = alloc(one, "half", [P, 3], f32)
            nhalf = alloc(one, "nhalf", [P, 3], f32)
            gu_scale = alloc(one, "gu_scale", [P, 1], f32)

            NWT = 4 * KT
            NTT = 4
            RING = 6

            def bank_of(p):
                return banks[2 + p % RING]

            def emptied(c, p):
                if p >= RING:
                    return evacuated(c, p - RING)
                before = max(b for b in range(TILES) if b % RING == p % RING)
                return c * TILES + before + 1

            def dve_normalise(dve, c, stage):
                base = c * LN_STEPS
                if stage == 0:
                    dve.wait_ge(x_loaded, c * 16 + 16)
                    for t in range(TT):
                        nc.vector.bn_stats(stats[:, t, :], xin[:, t, :]).then_inc(ln_step, 1)
                if stage == 1:
                    for t in range(TT):
                        nc.vector.bn_aggr(moments[:, t, :], stats[:, t, :]).then_inc(ln_step, 1)
                if stage == 2:
                    dve.wait_ge(ln_step, base + 8)
                    nc.vector.tensor_scalar(var_eps[:], moments[:, :, 1], EPS, None, ALU.add).then_inc(ln_step, 1)
                if stage == 3:
                    dve.wait_ge(std_done, c + 1)
                    nc.vector.reciprocal(rstd0[:], std[:]).then_inc(ln_step, 1)
                    dve.wait_ge(ln_step, base + 10)
                    nc.vector.tensor_tensor(newton[:, 0], var_eps[:], rstd0[:], ALU.mult).then_inc(ln_step, 1)
                    dve.wait_ge(ln_step, base + 11)
                    nc.vector.scalar_tensor_tensor(out=newton[:, 1], in0=newton[:, 0], scalar=-0.5, in1=rstd0[:],
                                                   op0=ALU.mult, op1=ALU.mult).then_inc(ln_step, 1)
                    dve.wait_ge(ln_step, base + 12)
                    nc.vector.scalar_tensor_tensor(out=rstd[:], in0=newton[:, 1], scalar=1.5, in1=rstd0[:],
                                                   op0=ALU.add, op1=ALU.mult).then_inc(ln_step, 1)
                if stage == 4:
                    dve.wait_ge(ln_step, base + 13)
                    for t in range(TT):
                        nc.vector.tensor_scalar(xin[:, t, :], xin[:, t, :], moments[:, t, 0:1], rstd[:, t:t + 1],
                                                ALU.subtract, ALU.mult).then_inc(ln_step, 1)

            def act_root(act, c):
                act.wait_ge(ln_step, c * LN_STEPS + 9)
                nc.scalar.activation(std[:], var_eps[:], ACT.Sqrt).then_inc(std_done, 1)

            def pe_transpose(pe, c, kt):
                if kt >= 2:
                    pe.wait_ge(xl_done, c * 2 * KT + 2 * (kt - 1))
                for t in range(TT):
                    last = nc.tensor.transpose(banks[kt % 2][:, t * P:(t + 1) * P], xin[:, t, kt * P:(kt + 1) * P], identf[:])
                last.then_inc(xt_done, 1)

            def act_split(act, c, kt):
                act.wait_ge(xt_done, c * KT + kt + 1)
                nc.scalar.activation(XH[:, kt, :], banks[kt % 2], ACT.Identity).then_inc(xh_done, 1)
                nc.scalar.activation(X16H[:, kt, :], banks[kt % 2], ACT.Identity, scale=X_SCALE).then_inc(xh_done, 1)

            def dve_split(dve, c, kt):
                dve.wait_ge(xh_done, c * 2 * KT + 2 * kt + 2)
                nc.vector.tensor_tensor(XL[:, kt, :], banks[kt % 2], XH[:, kt, :].bitcast(f32), ALU.subtract).then_inc(xl_done, 1)
                nc.vector.scalar_tensor_tensor(out=X16L[:, kt, :], in0=banks[kt % 2], scalar=X_SCALE, in1=X16H[:, kt, :],
                                               op0=ALU.mult, op1=ALU.subtract).then_inc(xl_done, 1)

            def weight(n):
                og, kt = divmod(n, KT)
                if og < 3:
                    return og, kt, WH[:, kt, og * D:(og + 1) * D], WL[:, kt, og * D:(og + 1) * D]
                return og, kt, OH[:, kt, :], OL[:, kt, :]

            def k_of(t):
                return (t * P + hidden_rows(t) - 1) // HO

            block = one.enter_context(nc.Block())

            @block.sync
            def _(sp):
                def load_weight(og):
                    src = w_qkv[og * D:(og + 1) * D, :] if og < 3 else w_out
                    sp.dma_start(wslot[og % 2], src.rearrange("(t p) d -> p t d", p=P)).then_inc(w_loaded[og % 2], 16)

                def store_qkv(c):
                    for m in range(2 * KT):
                        scr = q_scr if m < KT else k_scr
                        sp.wait_ge(q3_done, c * 2 * KT + m + 1)
                        sp.dma_start(scr[bass.ds(c // 2, 1), :, (m % KT) * P:(m % KT + 1) * P, bass.ds(c % 2 * CH, CH)].rearrange("a r p t -> p (a r) t"),
                                     qk_stage[m % 2][:]).then_inc(qk_stored[m % 2], 16)
                    for t in range(TT):
                        sp.wait_ge(evac_done, evacuated(c, V0 + t))
                        sp.dma_start(v_scr[bass.ds(c * CH + t * P, P), :], v_stage[t % 2][:]).then_inc(v_stored[t % 2], 16)

                def chunk(c):
                    sp.wait_ge(xt_done, c * KT + KT)
                    sp.dma_start(xin[:], xf[bass.ds((c + 1) * CH, CH), :].rearrange("(t p) d -> p t d", p=P)).then_inc(x_loaded, 16)
                    store_qkv(c)
                    sp_gated(sp, c)

                sp.dma_start(xin[:], xf[0:CH, :].rearrange("(t p) d -> p t d", p=P)).then_inc(x_loaded, 16)
                load_weight(0)
                load_weight(1)
                for og in (2, 3):
                    sp.wait_ge(wt_done, (og - 1) * KT)
                    load_weight(og)
                with sp.Fori(0, LAST) as c:
                    chunk(c)
                store_qkv(LAST)
                for i in range(2):
                    sp.wait_ge(qk_stored[i], NCH * KT * 16 + 16)
                    sp.wait_ge(v_stored[i], NCH * TT // 2 * 16 + 16)

            @block.gpsimd
            def _(pool):
                for w, src in enumerate((w_gate, w_up)):
                    for g in range(2):
                        pool.dma_start(GN[:, w, g], src[:, g * GRP:(g + 1) * GRP, :].rearrange("j p d -> p j d")
                                       ).then_inc(ffn_loaded, 16)
                for r in range(2):
                    pool.dma_start(DN[DO * r:DO * (r + 1)], w_down.rearrange("j o d -> o j d")).then_inc(ffn_loaded, 16)
                pool.dma_start(bq_col[:], b_qkv[0:2 * D].rearrange("(t p) -> p t", p=P),
                               allow_slow_non_contiguous=True).then_inc(bias_loaded, 16)
                pool.dma_start(bv_row[:], b_qkv[2 * D:3 * D].partition_broadcast(P)).then_inc(bias_loaded, 16)
                nc.gpsimd.memset(identf[:], 0.0).then_inc(s_const, 1)
                nc.gpsimd.memset(identb[:], 0.0).then_inc(s_const, 1)
                nc.gpsimd.memset(causal[:], 0.0).then_inc(s_const, 1)
                nc.gpsimd.memset(ones[:], 1.0).then_inc(s_const, 1)
                pool.wait_ge(s_const, 4)
                nc.gpsimd.affine_select(out=identf[:], in_=identf[:], compare_op=ALU.not_equal, fill=1.0, base=0,
                                        pattern=[[-1, P]], channel_multiplier=1).then_inc(s_const, 1)
                nc.gpsimd.affine_select(out=identb[:], in_=identb[:], compare_op=ALU.not_equal, fill=1.0, base=0,
                                        pattern=[[-1, P]], channel_multiplier=1).then_inc(s_const, 1)
                nc.gpsimd.affine_select(out=causal[:], in_=causal[:], compare_op=ALU.is_ge, fill=MASKED, base=0,
                                        pattern=[[-1, P]], channel_multiplier=1).then_inc(s_const, 1)
                nc.gpsimd.memset(primer[:, 0:1], 0.0).then_inc(evac_done, TILES)
                for i in range(2):
                    for n, ring in enumerate((qk_stored, v_stored, g_stored)):
                        nc.gpsimd.memset(primer[:, 1 + 3 * i + n:2 + 3 * i + n], 0.0).then_inc(ring[i], 16)

                def third(c):
                    for m in range(2 * KT):
                        pool.wait_ge(q2_done, c * 2 * KT + m + 1)
                        nc.gpsimd.tensor_tensor(qk_stage[m % 2][:, 2, :], rest[m % 2][:], qk_stage[m % 2][:, 1, :],
                                                ALU.subtract).then_inc(q3_done, 1)

                third(0)
                pool.wait_ge(mdn_done, OC * OC)
                pool_gated(pool, 0)
                with pool.Fori(1, LAST) as c:
                    third(c)
                    pool_gated(pool, c)
                third(LAST)

            @block.scalar
            def _(act):
                def first(c, behind=lambda m: None):
                    for m in range(2 * KT):
                        act.wait_ge(tile_done, c * TILES + QK0 + m + 1)
                        act.wait_ge(qk_stored[m % 2], c * (KT * 16) + m // 2 * 16 + 16)
                        nc.scalar.activation(qk_stage[m % 2][:, 0, :], bank_of(QK0 + m), ACT.Identity,
                                             bias=bq_col[:, m:m + 1]).then_inc(q1_done, 1)
                        behind(m)

                def place_down(i):
                    if i == 0:
                        act.wait_ge(tern_dn, 1)
                    for k in range(OC):
                        j, sign = OCT[k][i]
                        rows = slice(DO * (k % 2), DO * (k % 2 + 1))
                        nc.scalar.mul(MDn[rows, k // 2, i, :], dtern[rows, j, :], sign).then_inc(mdn_done, 1)

                def beside_of(c):
                    def beside(p):
                        if p == GU0 + 2 * (LN_AT[2] + 1):
                            act_root(act, c + 1)
                        if DN0 <= p < DN0 + 2:
                            act_split(act, c + 1, 2 * (p - DN0))
                            act_split(act, c + 1, 2 * (p - DN0) + 1)
                    return beside

                act_root(act, 0)
                for kt in range(KT):
                    act_split(act, 0, kt)
                for n in range(NWT):
                    act.wait_ge(wt_done, n + 1)
                    nc.scalar.activation(weight(n)[2], banks[2 + n % RING], ACT.Identity).then_inc(wh_done, 1)
                act.wait_ge(bias_loaded, 32)
                first(0, place_down)
                for n in range(NTT):
                    w, jq = divmod(n, 2)
                    act.wait_ge(tt_done, n + 1)
                    src = banks[n % 2].bitcast(bf16)[:, 0:OC * (GRP + 1)].rearrange("p (j g o) -> p j g o", g=2, o=GRP + 1)
                    nc.scalar.activation(TTs[:, w, jq * (OC // 2):(jq + 1) * (OC // 2), :].rearrange("p j (g o) -> p j g o", g=2),
                                         src[:, :, :, 0:GRP], ACT.Identity).then_inc(tt_copied, 1)

                later = beside_of(0)

                def beside(p):
                    t = (p - GU0) // 2
                    if GU0 <= p < DN0:
                        if t >= 1:
                            copy_down(t - 1)
                        if t == HT - 1:
                            copy_down(t)
                    later(p)

                def copy_down(m):
                    rows = hidden_rows(m)
                    act.wait_ge(mdt_done, m + 1)
                    nc.scalar.activation(MD[0:rows, m, :], banks[m % 2][0:rows].bitcast(bf16)[:, 0:D], ACT.Identity).then_inc(md_done, 1)

                act_gated(act, 0, bank_of, beside)
                with act.Fori(1, LAST) as c:
                    first(c)
                    act_gated(act, c, bank_of, beside_of(c))
                first(LAST)

            @block.vector
            def _(dve):
                chain = [0]

                def link(ins):
                    chain[0] += 1
                    ins.then_inc(dve_prep, 1)
                    dve.wait_ge(dve_prep, chain[0])

                def qkv(c):
                    for m in range(2 * KT):
                        dve.wait_ge(q1_done, c * 2 * KT + m + 1)
                        nc.vector.scalar_tensor_tensor(out=rest[m % 2][:], in0=bank_of(QK0 + m), scalar=bq_col[:, m:m + 1],
                                                       in1=qk_stage[m % 2][:, 0, :], op0=ALU.add, op1=ALU.subtract).then_inc(evac_done, 1)
                        dve.wait_ge(evac_done, evacuated(c, QK0 + m))
                        nc.vector.tensor_copy(qk_stage[m % 2][:, 1, :], rest[m % 2][:]).then_inc(q2_done, 1)
                    for t in range(TT):
                        dve.wait_ge(tile_done, c * TILES + V0 + t + 1)
                        dve.wait_ge(v_stored[t % 2], c * (TT // 2 * 16) + t // 2 * 16 + 16)
                        nc.vector.tensor_tensor(v_stage[t % 2][:].rearrange("p (q d h) -> p q h d", q=NQ, h=QH),
                                                bank_of(V0 + t).rearrange("p (q h d) -> p q h d", q=NQ, h=QH),
                                                bv_row[:].rearrange("p (q h d) -> p q h d", q=NQ, h=QH), ALU.add).then_inc(evac_done, 1)

                def beside_of(c):
                    def beside(p):
                        if GU0 <= p < DN0:
                            t, up = divmod(p - GU0, 2)
                            if up and t in LN_AT:
                                dve_normalise(dve, c + 1, LN_AT.index(t))
                            if not up and t == LN_AT[1]:
                                dve.wait_ge(ln_step, (c + 1) * LN_STEPS + 4)
                        if DN0 <= p < DN0 + 2:
                            dve_split(dve, c + 1, 2 * (p - DN0))
                            dve_split(dve, c + 1, 2 * (p - DN0) + 1)
                    return beside

                nc.vector.memset(asum[:], 0.0).then_inc(asum_done, 1)
                for stage in range(5):
                    if stage == 1:
                        dve.wait_ge(ln_step, 4)
                    dve_normalise(dve, 0, stage)
                for kt in range(KT):
                    dve_split(dve, 0, kt)
                dve.wait_ge(ffn_loaded, 6 * 16)
                dve.wait_ge(asum_done, 1)
                for w in range(2):
                    link(nc.vector.tensor_reduce(asum[0:GRP, w:w + 1], GN[:, w].rearrange("p g j d -> p (g j d)"), AX.X, ALU.add,
                                                 apply_absolute_value=True))
                nc.vector.tensor_reduce(asum[0:DO, 2:3], DN[0:DO].rearrange("p j d -> p (j d)"), AX.X, ALU.add,
                                        apply_absolute_value=True).then_inc(asum_done, 2)
                for n in range(NWT):
                    dve.wait_ge(wh_done, n + 1)
                    og, kt, hi, lo = weight(n)
                    nc.vector.tensor_tensor(lo, banks[2 + n % RING], hi.bitcast(f32), ALU.subtract).then_inc(wl_done, 1)
                dve.wait_ge(mean_ready, 1)
                link(nc.vector.tensor_scalar(mean[:], banks[0][:, 0:3], 1.0 / (OC * HO * DO), None, ALU.mult))
                nc.vector.tensor_scalar(half[:], mean[:], 0.5, None, ALU.mult)
                nc.vector.tensor_scalar(sig_scale[:], mean[:, 0:1], 1.0 / X_SCALE, None, ALU.mult)
                link(nc.vector.tensor_tensor(gu_scale[:], mean[:, 0:1], mean[:, 1:2], ALU.mult))
                link(nc.vector.tensor_scalar(ffn_scale[:], gu_scale[:], mean[:, 2:3], 1.0 / (X_SCALE * X_SCALE * H_SCALE), ALU.mult, ALU.mult))
                link(nc.vector.tensor_scalar(nhalf[:], mean[:], -0.5, None, ALU.mult))
                for w in range(2):
                    if w:
                        dve.wait_ge(tern_gu, w)
                    link(nc.vector.tensor_scalar(gneg, GN[:, w].rearrange("p g j d -> p (g j d)"), nhalf[0:GRP, w:w + 1], None, ALU.is_lt))
                    nc.vector.scalar_tensor_tensor(out=gtern[:, w].rearrange("p g j d -> p (g j d)"),
                                                   in0=GN[:, w].rearrange("p g j d -> p (g j d)"), scalar=half[0:GRP, w:w + 1], in1=gneg,
                                                   op0=ALU.is_gt, op1=ALU.subtract).then_inc(tern_gu, 1)
                link(nc.vector.tensor_scalar(dneg, DN, nhalf[:, 2:3], None, ALU.is_lt))
                nc.vector.scalar_tensor_tensor(out=dtern, in0=DN, scalar=half[:, 2:3], in1=dneg,
                                               op0=ALU.is_gt, op1=ALU.subtract).then_inc(tern_dn, 1)
                dve.wait_ge(bias_loaded, 32)
                qkv(0)
                dve.wait_ge(tt_copied, NTT)
                for k in range(OC):
                    for i in range(OC):
                        j, sign = OCT[k][i]
                        rows = slice(DO * (i % 2), DO * (i % 2 + 1))
                        last = nc.vector.tensor_scalar(MG[rows, i // 2, :, k * HO:(k + 1) * HO], TTs[rows, :, j, :], sign, None, ALU.mult)
                    last.then_inc(mg_done, 1)
                dve_gated(dve, 0, bank_of, beside_of(0))
                with dve.Fori(1, LAST) as c:
                    qkv(c)
                    dve_gated(dve, c, bank_of, beside_of(c))
                qkv(LAST)

            @block.tensor
            def _(pe):
                def free(c, p):
                    pe.wait_ge(evac_done, emptied(c, p))

                def qk(c):
                    pe.wait_ge(xl_done, c * 2 * KT + 2 * KT)
                    for m in range(2 * KT):
                        cols = slice(m * P, (m + 1) * P)
                        free(c, QK0 + m)
                        for kt in range(KT):
                            nc.tensor.matmul(bank_of(QK0 + m), WH[:, kt, cols], XH[:, kt, :], start=(kt == 0), stop=False)
                            nc.tensor.matmul(bank_of(QK0 + m), WH[:, kt, cols], XL[:, kt, :], start=False, stop=False)
                            last = nc.tensor.matmul(bank_of(QK0 + m), WL[:, kt, cols], XH[:, kt, :], start=False, stop=(kt == KT - 1))
                        last.then_inc(tile_done, 1)

                def v(c):
                    for t in range(TT):
                        tok, cols = slice(t * P, (t + 1) * P), slice(2 * D, 3 * D)
                        free(c, V0 + t)
                        for kt in range(KT):
                            nc.tensor.matmul(bank_of(V0 + t), XH[:, kt, tok], WH[:, kt, cols], start=(kt == 0), stop=False)
                            nc.tensor.matmul(bank_of(V0 + t), XH[:, kt, tok], WL[:, kt, cols], start=False, stop=False)
                            last = nc.tensor.matmul(bank_of(V0 + t), XL[:, kt, tok], WH[:, kt, cols], start=False, stop=(kt == KT - 1))
                        last.then_inc(tile_done, 1)

                def beside_of(c):
                    def beside(p):
                        if p == DN0:
                            pe.wait_ge(ln_step, c * LN_STEPS + 2 * LN_STEPS)
                        if DN0 <= p < DN0 + 2:
                            pe_transpose(pe, c + 1, 2 * (p - DN0))
                            pe_transpose(pe, c + 1, 2 * (p - DN0) + 1)
                    return beside

                pe.wait_ge(s_const, 7)
                pe.wait_ge(ln_step, LN_STEPS)
                for kt in range(KT):
                    pe_transpose(pe, 0, kt)
                for n in range(NWT):
                    og, kt, _, _ = weight(n)
                    if kt == 0:
                        pe.wait_ge(w_loaded[og % 2], og // 2 * 16 + 16)
                    if n >= RING:
                        pe.wait_ge(wl_done, n - RING + 1)
                    for t in range(TT):
                        last = nc.tensor.transpose(banks[2 + n % RING][:, t * P:(t + 1) * P], wslot[og % 2][:, t, kt * P:(kt + 1) * P], identf[:])
                    last.then_inc(wt_done, 1)
                pe.wait_ge(asum_done, 3)
                pe.wait_ge(xl_done, 2 * KT)
                nc.tensor.matmul(banks[0][:, 0:3], ones[:], asum[:], start=True, stop=True).then_inc(mean_ready, 1)
                pe.wait_ge(wl_done, NWT)
                qk(0)
                pe.wait_ge(tern_gu, 2)
                for n in range(NTT):
                    w, jq = divmod(n, 2)
                    if n >= 2:
                        pe.wait_ge(tt_copied, n - 1)
                    dst = banks[n % 2].bitcast(bf16)
                    for jj in range(OC // 2):
                        for g in range(2):
                            at = (jj * 2 + g) * (GRP + 1)
                            for r in range(2):
                                last = nc.tensor.transpose(dst[DO * r:DO * (r + 1), at:at + GRP],
                                                           gtern[:, w, g, jq * (OC // 2) + jj, :], identb[0:GRP, 0:GRP])
                    last.then_inc(tt_done, 1)
                v(0)

                mdn = MDn.rearrange("p k i d -> p k (i d)")
                later = beside_of(0)

                def transpose_down(m):
                    if m >= 2:
                        pe.wait_ge(md_done, m - 1)
                    dst = banks[m % 2].bitcast(bf16)
                    for k in range(OC // 2):
                        last = nc.tensor.transpose(dst[0:hidden_rows(m), k * P:(k + 1) * P],
                                                   mdn[:, k, m * P:m * P + hidden_rows(m)], identb[:])
                    last.then_inc(mdt_done, 1)

                def beside(p):
                    if GU0 <= p < DN0:
                        t, up = divmod(p - GU0, 2)
                        if not up:
                            transpose_down(t)
                            if t + 1 < HT:
                                pe.wait_ge(mg_done, k_of(t + 1) + 1)
                        elif t == HT - 1:
                            pe.wait_ge(md_done, HT)
                    later(p)

                pe.wait_ge(mdn_done, OC * OC)
                pe.wait_ge(mg_done, k_of(0) + 1)
                pe_gated(pe, 0, bank_of, free, beside)
                with pe.Fori(1, LAST) as c:
                    qk(c)
                    v(c)
                    pe_gated(pe, c, bank_of, free, beside_of(c))
                qk(LAST)
                v(LAST)

        two = ExitStack()
        with two:
            Qs = [alloc(two, f"Qs{i}", [P, QH, S], bf16) for i in range(SLOTS)]
            Ks = [alloc(two, f"Ks{i}", [P, QH, S], bf16) for i in range(SLOTS)]
            Vs = [alloc(two, f"Vs{i}", [P, KB, 2 * QH * HD], f32) for i in range(SLOTS)]
            probs = [alloc(two, f"probs{i}", [P, QH, CH], f32) for i in range(PSLOTS)]
            mx = [alloc(two, f"mx{i}", [P, QH, KB], f32) for i in range(2)]
            mx2 = [alloc(two, f"mx2{i}", [P, QH, KB // 2], f32) for i in range(2)]
            mrest = alloc(two, "mrest", [P, QH * KB], f32)
            mparts = alloc(two, "mparts", [P, 3, QH * KB], bf16)
            mrows = alloc(two, "mrows", [3 * QH * KB, P], bf16)
            osum = [alloc(two, f"osum{i}", [P, CH], f32) for i in range(2)]

            fixed = sem("fixed")
            stacked = [sem(f"stacked{i}") for i in range(SLOTS)]
            max_filled = sem("max_filled")
            max_read = sem("max_read")
            max_step = sem("max_step")
            mt_filled = sem("mt_filled")
            mt_copied = sem("mt_copied")
            m_stacked = sem("m_stacked")
            s_filled = sem("s_filled")
            exp_done = sem("exp_done")
            pv_done = sem("pv_done")
            o_copied = sem("o_copied")
            o_stored = [sem(f"o_stored{i}") for i in range(2)]

            NLOAD = 2 * len(TERM_Q) + 2
            MSTEP = 5
            s_bank = [psum[:, 0:2, :], psum[:, 2:4, :]]
            m_bank = [banks[4], banks[5]]
            pv_bank, mt_bank = banks[6], banks[7]
            gated_banks = [banks[i] for i in (0, 1, 2, 3, 6)]
            FRING = len(gated_banks)
            early = [(0, j) for j in range(NMAX)] + [(1, j) for j in range(LEAD)]
            EARLY_PER_TILE = 2

            def gated_bank(p):
                return gated_banks[(p - GU0) % FRING]

            def early_beside(p):
                at = (p - GU0) * EARLY_PER_TILE
                return early[at:at + EARLY_PER_TILE]

            def stack_uses(t, s):
                return ((t - s) // SLOTS + 1) * NLOAD * 16

            block = two.enter_context(nc.Block())

            @block.sync
            def _(sp):
                def load(t, s, free):
                    if free:
                        sp.wait_ge(pv_done, (t - SLOTS) * NST + NST + PSLOTS)
                    b, hq = t // NQ, t % NQ
                    for n, (qp, kp) in enumerate(zip(TERM_Q, TERM_K)):
                        rows = slice(n * HD, (n + 1) * HD)
                        for dst, scr, part in ((Qs, q_scr, qp), (Ks, k_scr, kp)):
                            sp.dma_start(dst[s][rows], scr[bass.ds(b, 1), part, bass.ds(hq * (QH * HD), QH * HD)].rearrange("a (h d) t -> d (a h) t", d=HD)
                                         ).then_inc(stacked[s], 16)
                    sp.dma_start(Ks[s][ROWS_QK:ROWS_MAX], alibi[bass.ds(hq * QH, QH)].rearrange("h r t -> r h t")).then_inc(stacked[s], 16)
                    sp.dma_start(Vs[s][:, :, 0:QH * HD], v_scr[bass.ds(b * S, S), bass.ds(hq * (QH * HD), QH * HD)].rearrange("(k p) c -> p k c", p=P)
                                 ).then_inc(stacked[s], 16)

                def maximum(t, s):
                    sp.wait_ge(mt_copied, t + 1)
                    sp.dma_start(Qs[s][ROWS_MAX:ROWS_ALL], mrows[:]).then_inc(m_stacked, 16)

                def store(t, c):
                    sp.wait_ge(o_copied, t * 2 + c + 1)
                    sp.dma_start(o_scr[bass.ds(t // NQ, 1), c, bass.ds(t % NQ, 1)].rearrange("a b p t -> p (a b) t"), osum[c][:]
                                 ).then_inc(o_stored[c], 16)

                def step(t, s, ahead, lead):
                    if lead:
                        load(t + 2, (s + 2) % SLOTS, True)
                    store(t, 0)
                    if ahead:
                        maximum(t + 1, (s + 1) % SLOTS)
                    store(t, 1)

                sp.wait_ge(fixed, 3 * SLOTS)
                load(0, 0, False)
                load(1, 1, False)
                load(2, 2, False)
                sp_gated(sp, LAST)
                maximum(0, 0)
                store(0, 0)
                maximum(1, 1)
                store(0, 1)
                with sp.Fori(0, 4) as g:
                    for s in range(SLOTS):
                        step(g * SLOTS + s + 1, (s + 1) % SLOTS, True, True)
                step(13, 1, True, True)
                step(14, 2, True, False)
                step(15, 0, False, False)
                for c in range(2):
                    sp.wait_ge(o_stored[c], QUADS * 16 + 16)
                    sp.wait_ge(g_stored[c], NCH * TT // 2 * 16 + 16)

            @block.gpsimd
            def _(pool):
                for i in range(SLOTS):
                    nc.gpsimd.memset(Qs[i][ROWS_QK:P], 1.0).then_inc(fixed, 1)
                    nc.gpsimd.memset(Ks[i][ROWS_QK:P], 1.0).then_inc(fixed, 1)
                pool.wait_ge(fixed, 2 * SLOTS)
                for i in range(SLOTS):
                    nc.gpsimd.memset(Vs[i][:, :, QH * HD:], 1.0).then_inc(fixed, 1)
                for n, (ring, count) in enumerate(((exp_done, 2), (max_read, 2), (pv_done, PSLOTS), (mt_filled, 1), (m_stacked, 16),
                                                   (o_stored[0], 16), (o_stored[1], 16))):
                    nc.gpsimd.memset(primer[:, n:n + 1], 0.0).then_inc(ring, count)
                pool_gated(pool, LAST)

            @block.scalar
            def _(act):
                def step(t):
                    for n in range(NST):
                        for pair in range(2):
                            act.wait_ge(s_filled, t * (2 * NST) + 2 * n + pair + 1)
                            act.wait_ge(pv_done, t * NST + n + 1)
                            nc.scalar.activation(probs[n % PSLOTS][:, 2 * pair:2 * pair + 2, 0:COLS[n]], s_bank[pair][:, :, 0:COLS[n]],
                                                 ACT.Exp, scale=1.0 / INV_SCALE).then_inc(exp_done, 1)
                        if n == 4 + LAG - 1:
                            copy_out(t, 0, 3)
                    copy_out(t, 1, NST - 1)

                def copy_out(t, c, n):
                    act.wait_ge(pv_done, t * NST + n + 1 + PSLOTS)
                    act.wait_ge(o_stored[c], t * 16 + 16)
                    nc.scalar.activation(osum[c][:], pv_bank, ACT.Copy).then_inc(o_copied, 1)

                act_gated(act, LAST, gated_bank, lambda p: None)
                with act.Fori(0, QUADS) as t:
                    step(t)

            @block.vector
            def _(dve):
                def read_max(t, j, s):
                    qb, h, n, k0, keys = MAXT[j]
                    dve.wait_ge(max_filled, t * NMAX + j + 1)
                    dst = mx[s][:, h:h + n, qb:qb + 1] if k0 == 0 else mx2[s][:, h:h + n, qb - 4:qb - 3]
                    nc.vector.tensor_reduce(dst, m_bank[j % 2][:, 0:n * keys].rearrange("p (n k) -> p n k", n=n), AX.X, ALU.max
                                            ).then_inc(max_read, 1)

                def parts(t, s):
                    dve.wait_ge(max_read, t * NMAX + NMAX + 2)
                    nc.vector.tensor_tensor(mx[s][:, :, 4:8], mx[s][:, :, 4:8], mx2[s][:], ALU.max).then_inc(max_step, 1)
                    flat = mx[s][:].rearrange("p h q -> p (h q)")
                    dve.wait_ge(max_step, t * MSTEP + 1)
                    dve.wait_ge(mt_filled, t + 1)
                    nc.vector.tensor_scalar(mparts[:, 0, :], flat, -1.0, None, ALU.mult).then_inc(max_step, 1)
                    dve.wait_ge(max_step, t * MSTEP + 2)
                    nc.vector.scalar_tensor_tensor(out=mrest[:], in0=flat, scalar=-1.0, in1=mparts[:, 0, :], op0=ALU.mult,
                                                   op1=ALU.subtract).then_inc(max_step, 1)
                    dve.wait_ge(max_step, t * MSTEP + 3)
                    nc.vector.tensor_copy(mparts[:, 1, :], mrest[:]).then_inc(max_step, 1)
                    dve.wait_ge(max_step, t * MSTEP + 4)
                    nc.vector.tensor_tensor(mparts[:, 2, :], mrest[:], mparts[:, 1, :], ALU.subtract).then_inc(max_step, 1)

                def rows(t):
                    dve.wait_ge(mt_filled, t + 2)
                    dve.wait_ge(m_stacked, t * 16 + 16)
                    nc.vector.tensor_copy(mrows[:], mt_bank[0:3 * QH * KB, 0:P // 2].bitcast(bf16)).then_inc(mt_copied, 1)

                def finish(t, s):
                    parts(t, s)
                    rows(t)

                def beside(p):
                    for t, j in early_beside(p):
                        read_max(t, j, t % 2)
                        if (t, j) == (0, NMAX - 1):
                            finish(0, 0)

                dve_gated(dve, LAST, gated_bank, beside)
                for j in range(LEAD, NMAX):
                    read_max(1, j, 1)
                finish(1, 1)
                with dve.Fori(1, QUADS // 2) as g:
                    for s in range(2):
                        t = g * 2 + s
                        for j in range(NMAX):
                            read_max(t, j, s)
                        finish(t, s)

            @block.tensor
            def _(pe):
                def fill_max(t, j, s):
                    qb, h, n, k0, keys = MAXT[j]
                    if j == 0:
                        pe.wait_ge(stacked[s], stack_uses(t, s))
                    pe.wait_ge(max_read, t * NMAX + j + 1)
                    masked = k0 + keys == (qb + 1) * P
                    for i in range(n):
                        dst = m_bank[j % 2][:, i * keys:(i + 1) * keys]
                        last = nc.tensor.matmul(dst, Qs[s][0:ROWS_MAX, h + i, qb * P:(qb + 1) * P], Ks[s][0:ROWS_MAX, h + i, k0:k0 + keys],
                                                start=True, stop=not masked)
                        if masked:
                            last = nc.tensor.matmul(dst[:, keys - P:keys], identb[:], causal[:], start=False, stop=True)
                    last.then_inc(max_filled, 1)

                def transpose_max(t):
                    pe.wait_ge(max_step, t * MSTEP + MSTEP)
                    nc.tensor.transpose(mt_bank[0:3 * QH * KB, 0:P // 2].bitcast(bf16), mparts[:].rearrange("p r n -> p (r n)"), identb[:]
                                        ).then_inc(mt_filled, 1)

                def scores(t, n, pair, s):
                    c, kb = STEPS[n]
                    pe.wait_ge(exp_done, t * (2 * NST) + 2 * n + pair + 1)
                    for h in range(2):
                        last = nc.tensor.matmul(s_bank[pair][:, h, 0:COLS[n]], Ks[s][0:ROWS_ALL, 2 * pair + h, kb * P:(kb + 1) * P],
                                                Qs[s][0:ROWS_ALL, 2 * pair + h, (c + 1) * CH - COLS[n]:(c + 1) * CH], start=True, stop=not DIAG[n])
                        if DIAG[n]:
                            last = nc.tensor.matmul(s_bank[pair][:, h, 0:P], causal[:], identb[:], start=False, stop=True)
                    last.then_inc(s_filled, 1)

                def products(t, n, s):
                    c, kb = STEPS[n]
                    pe.wait_ge(exp_done, t * (2 * NST) + 2 * n + 2 + 2)
                    if kb == 0 and not (isinstance(t, int) and t == 0 and c == 0):
                        pe.wait_ge(o_copied, t * 2 + c)
                    for h in range(QH):
                        last = nc.tensor.matmul(pv_bank[32 * h:32 * h + 32, CH - COLS[n]:CH], Vs[s][:, kb, h::QH],
                                                probs[n % PSLOTS][:, h, 0:COLS[n]], start=(kb == 0), stop=(kb == 4 * c + 3))
                    last.then_inc(pv_done, 1)

                def step(t, s, ahead, lead):
                    pe.wait_ge(m_stacked, t * 16 + 32)
                    for kind, a, b in interleave(ahead, lead):
                        if kind == "scores":
                            scores(t, a, b, s)
                        elif kind == "products":
                            products(t, a, s)
                        else:
                            fill_max(t + a, b, (s + a) % SLOTS)
                            if (a, b) == ((2, 1) if lead else (1, NMAX - 1)):
                                transpose_max(t + 1)

                def free(c, p):
                    if p - GU0 >= FRING:
                        pe.wait_ge(evac_done, evacuated(c, p - FRING))

                def beside(p):
                    for t, j in early_beside(p):
                        fill_max(t, j, t)
                        if (t, j) == (1, 1):
                            transpose_max(0)

                pe.wait_ge(fixed, 3 * SLOTS)
                pe_gated(pe, LAST, gated_bank, free, beside)
                step(0, 0, True, True)
                with pe.Fori(0, 4) as g:
                    for s in range(SLOTS):
                        step(g * SLOTS + s + 1, (s + 1) % SLOTS, True, True)
                step(13, 1, True, True)
                step(14, 2, True, False)
                step(15, 0, False, False)

        ffn.close()

        three = ExitStack()
        with three:
            bo_row = alloc(three, "bo_row", [P, D], f32)
            den = alloc(three, "den", [P, CH], f32)
            rec = [alloc(three, f"rec{i}", [P, KT, CH], f32) for i in range(2)]
            num = [alloc(three, f"num{i}", [P, KT, CH], f32) for i in range(2)]
            AH = [alloc(three, f"AH{i}", [P, KT, CH], f32r) for i in range(2)]
            AL = [alloc(three, f"AL{i}", [P, KT, CH], f32r) for i in range(2)]
            gate = [alloc(three, f"gate{i}", [P, TT, D], f32) for i in range(2)]
            xres = [alloc(three, f"xres{i}", [P, TT, D], f32) for i in range(2)]
            scaled = [alloc(three, f"scaled{i}", [P, D], f32) for i in range(2)]
            fin = alloc(three, "fin", [P, NCH * TT, D], f32)

            bo_loaded = sem("bo_loaded")
            den_loaded = sem("den_loaded")
            den_done = sem("den_done")
            rec_stored = sem("rec_stored")
            sums_loaded = [sem(f"sums_loaded{i}") for i in range(2)]
            tok_loaded = [sem(f"tok_loaded{i}") for i in range(2)]
            att_done = sem("att_done")
            ah_done = sem("ah_done")
            al_done = sem("al_done")
            proj_done = sem("proj_done")
            proj_read = sem("proj_read")
            gated_done = sem("gated_done")
            fin_done = sem("fin_done")
            fin_stored = sem("fin_stored")
            TOK_LOADS, SUM_LOADS = 2, 4 * KT

            block = three.enter_context(nc.Block())

            @block.sync
            def _(sp):
                sp.dma_start(den[:], o_scr.rearrange("b c q (h x d) t -> x d (b c q) h t", x=2, d=HD)[1, 0]).then_inc(den_loaded, 16)
                sp.dma_start(bo_row[:], b_out.partition_broadcast(P)).then_inc(bo_loaded, 16)
                sp.wait_ge(den_done, 1)
                sp.dma_start(r_scr.rearrange("b c q h t -> (b c q h) t"), den[:]).then_inc(rec_stored, 16)
                sp.wait_ge(rec_stored, 16)
                with sp.Fori(0, NCH // 2) as g:
                    for i in range(2):
                        sp.wait_ge(al_done, g * (2 * KT) + i * KT + KT)
                        for kt in range(KT):
                            for u in range(2):
                                rows = slice(QH * HD * u, QH * HD * (u + 1))
                                src = o_scr[bass.ds(g, 1), i, 2 * kt + u].rearrange("a (h x d) t -> x (a h) d t", x=2, d=HD)
                                sp.dma_start(num[i][rows, kt], src[0]).then_inc(sums_loaded[i], 16)
                                src = r_scr[bass.ds(g, 1), i, 2 * kt + u].rearrange("a h t -> (a h) t").unsqueeze(1)
                                sp.dma_start(rec[i][rows, kt], src.to_broadcast([QH, HD, CH])).then_inc(sums_loaded[i], 16)
                        sp.wait_ge(fin_done, g * (2 * TT) + i * TT + TT)
                        for dst, src in ((gate, g_scr), (xres, xf)):
                            sp.dma_start(dst[i][:], src[bass.ds(g * (2 * CH) + i * CH, CH), :].rearrange("(t p) d -> p t d", p=P)
                                         ).then_inc(tok_loaded[i], 16)

            @block.gpsimd
            def _(pool):
                for n, (ring, count) in enumerate(((al_done, 2 * KT), (fin_done, 2 * TT), (proj_read, 2 * TT), (proj_done, 2 * TT))):
                    nc.gpsimd.memset(primer[:, n:n + 1], 0.0).then_inc(ring, count)
                with pool.Fori(0, NCH // 2) as g:
                    for i in range(2):
                        for t in range(TT):
                            n = g * (2 * TT) + i * TT + t
                            pool.wait_ge(gated_done, n + 1)
                            nc.gpsimd.tensor_tensor(fin[:, bass.ds(n, 1), :].rearrange("p a d -> p (a d)"), scaled[t % 2][:], xres[i][:, t, :], ALU.add).then_inc(fin_done, 1)
                            pool.wait_ge(fin_done, n + 1 + 2 * TT)
                            pool.dma_start(outf[bass.ds(g * (2 * CH) + i * CH + t * P, P), :], fin[:, bass.ds(n, 1), :].rearrange("p a d -> p (a d)")).then_inc(fin_stored, 16)
                pool.wait_ge(fin_stored, NCH * TT * 16)

            @block.vector
            def _(dve):
                def prepare(c):
                    i = c % 2
                    dve.wait_ge(sums_loaded[i], (c // 2 + 1) * SUM_LOADS * 16)
                    for kt in range(KT):
                        nc.vector.tensor_tensor(num[i][:, kt, :], num[i][:, kt, :], rec[i][:, kt, :], ALU.mult).then_inc(att_done, 1)
                    for kt in range(KT):
                        dve.wait_ge(ah_done, c * KT + kt + 1)
                        nc.vector.tensor_tensor(AL[i][:, kt, :], num[i][:, kt, :], AH[i][:, kt, :].bitcast(f32), ALU.subtract).then_inc(al_done, 1)

                def finish(c):
                    i = c % 2
                    dve.wait_ge(tok_loaded[i], (c // 2 + 1) * TOK_LOADS * 16)
                    for t in range(TT):
                        n = c * TT + t
                        dve.wait_ge(proj_done, n + 1 + 2 * TT)
                        if n >= 2:
                            dve.wait_ge(fin_done, n - 1 + 2 * TT)
                        nc.vector.tensor_tensor(scaled[t % 2][:], banks[TT * i + t], bo_row[:], ALU.add).then_inc(proj_read, 1)
                        dve.wait_ge(proj_read, n + 1 + 2 * TT)
                        nc.vector.tensor_tensor(scaled[t % 2][:], scaled[t % 2][:], gate[i][:, t, :], ALU.mult).then_inc(gated_done, 1)

                dve.wait_ge(den_loaded, 16)
                nc.vector.reciprocal(den[:], den[:]).then_inc(den_done, 1)
                dve.wait_ge(bo_loaded, 16)
                prepare(0)
                for c in range(1, NCH):
                    prepare(c)
                    finish(c - 1)
                finish(NCH - 1)

            @block.scalar
            def _(act):
                with act.Fori(0, NCH // 2) as g:
                    for i in range(2):
                        act.wait_ge(proj_done, g * (2 * TT) + i * TT + TT)
                        for kt in range(KT):
                            act.wait_ge(att_done, g * (2 * KT) + i * KT + kt + 1)
                            nc.scalar.activation(AH[i][:, kt, :], num[i][:, kt, :], ACT.Copy).then_inc(ah_done, 1)

            @block.tensor
            def _(pe):
                with pe.Fori(0, NCH // 2) as g:
                    for i in range(2):
                        pe.wait_ge(al_done, g * (2 * KT) + i * KT + KT + 2 * KT)
                        for t in range(TT):
                            tok = slice(t * P, (t + 1) * P)
                            pe.wait_ge(proj_read, g * (2 * TT) + i * TT + t + 1)
                            for kt in range(KT):
                                nc.tensor.matmul(banks[TT * i + t], AH[i][:, kt, tok], OH[:, kt, :], start=(kt == 0), stop=False)
                                nc.tensor.matmul(banks[TT * i + t], AH[i][:, kt, tok], OL[:, kt, :], start=False, stop=False)
                                last = nc.tensor.matmul(banks[TT * i + t], AL[i][:, kt, tok], OH[:, kt, :], start=False, stop=(kt == KT - 1))
                            last.then_inc(proj_done, 1)


def alibi_parts():
    import numpy as np

    m = np.arange(1, H + 1, dtype=np.float32) * np.float32(8 / H)
    slopes = np.float32(1.0) / np.power(np.float32(2.0), m)
    rest = slopes[:, None] * np.arange(1 - S, 1, dtype=np.float32)[None, :] * np.float32(INV_SCALE)
    parts = []
    for _ in range(3):
        bits = rest.view(np.uint32) & np.uint32(0xFFFF0000)
        parts.append((bits >> 16).astype(np.uint16))
        rest = rest - bits.view(np.float32)
    return np.ascontiguousarray(np.stack(parts, axis=1))


_INS = ["L0_attn_x", "L0_attn_w_qkv", "L0_attn_b_qkv", "L0_attn_w_out", "L0_attn_b_out", "L0_ffn_w_gate", "L0_ffn_w_up", "L0_ffn_w_down"]


def kernel(**inputs):
    import numpy as np
    import concourse.bacc as bacc
    from concourse.bass_utils import run_bass_kernel_spmd

    nc = bacc.Bacc("TRN2", target_bir_lowering=False, num_devices=1)
    arrays = {f"in_{name}": np.ascontiguousarray(inputs[name]) for name in _INS}
    args = [nc.dram_tensor(n, a.shape, mybir.dt.from_np(a.dtype), kind="ExternalInput").ap() for n, a in arrays.items()]
    arrays["alibi"] = alibi_parts()
    alibi = nc.dram_tensor("alibi", arrays["alibi"].shape, mybir.dt.uint16, kind="ExternalInput").ap().bitcast(mybir.dt.bfloat16)
    out = nc.dram_tensor("out", (B, S, D), mybir.dt.float32, kind="ExternalOutput").ap()
    program(nc, *args, alibi, out)
    r = run_bass_kernel_spmd(nc, [arrays], core_ids=[0])
    return r.results[0]["out"]
```

```python
import concourse.bass as bass
from concourse import mybir
from contextlib import ExitStack

B, S, D, H = 2, 1024, 512, 32
HD = D // H
T = B * S
P = 128
KT = D // P
CH = 512
NCH = T // CH
TT = CH // P
OC = 8
HO, DO = 1366 // OC, D // OC
HID = OC * HO
HT = -(-HID // P)
GRP = HO // 2
EPS = 1e-5
TRIPLES = [(1, 2, 3), (1, 4, 5), (1, 7, 6), (2, 4, 6), (2, 5, 7), (3, 4, 7), (3, 6, 5)]

QH = 4
NQ = H // QH
QUADS = B * NQ
KB = S // P
TERM_Q = [0, 0, 1, 1, 0, 2]
TERM_K = [0, 1, 0, 1, 2, 0]
ROWS_QK = HD * len(TERM_Q)
ROWS_MAX = ROWS_QK + 3
ROWS_ALL = ROWS_MAX + 3
SLOTS = 3
INV_SCALE = 4.0
MASKED = -1.0e9 * INV_SCALE

X_SCALE = 256.0
H_SCALE = 2.0 ** -19


def octonion():
    by = [[None] * OC for _ in range(OC)]
    by[0][0] = (0, 1.0)
    for i in range(1, OC):
        by[i][i] = (0, 1.0)
        by[i][0] = (i, 1.0)
        by[0][i] = (i, -1.0)
    for a, b, c in TRIPLES:
        for x, y, z in ((a, b, c), (b, c, a), (c, a, b)):
            by[z][y] = (x, 1.0)
            by[z][x] = (y, -1.0)
    return by


OCT = octonion()

QK0, V0, GU0, DN0 = 0, 2 * KT, 2 * KT + TT, 2 * KT + TT + 2 * HT
TILES = DN0 + TT
LAST = NCH - 1
LN_AT = [1, 2, 3, 6, 7]
LN_STEPS = 4 + 4 + 1 + 4 + 4
NSIG = 3


def hidden_rows(t):
    return min(P, HID - t * P)


def max_tiles():
    out = []
    for half in range(2):
        for qb in range(4 * half, KB):
            keys = min(CH, P * (qb + 1) - CH * half)
            n = CH // keys
            for h in range(0, QH, n):
                out.append((qb, h, min(n, QH - h), CH * half, keys))
    return out


MRING = 3
MAXT = max_tiles()
NMAX = len(MAXT)
NITEM = NMAX + 1
ROWS_AT = 5


def steps():
    out = []
    for c in range(S // CH):
        out += [(c, [(kb, 0, CH)]) for kb in range(4 * c + 1)]
        out += [(c, [(4 * c + 2, 0, CH - 2 * P)]), (c, [(4 * c + 1, 0, CH - P), (4 * c + 3, CH - P, P)])]
    return out


STEPS = steps()
NST = len(STEPS)
COLS = [sum(w for _, _, w in blocks) for _, blocks in STEPS]
DIAG = [n for n, (c, blocks) in enumerate(STEPS) if blocks[0][0] >= 4 * c]
ENDS = [max(n for n, st in enumerate(STEPS) if st[0] == c) for c in range(S // CH)]
LEAD = 11
PARTS_COST = 900
LAST_PACE = 0.7
LAG = 3
PSLOTS = 5
LATE = [t % SLOTS for t in (QUADS - 3, QUADS - 2)]


def position(u, i):
    if isinstance(u, int) and u == 0:
        at = i - (i > ROWS_AT)
        return at, at % MRING
    if isinstance(u, int) and u == QUADS:
        return QUADS * NITEM - 1, (QUADS * NITEM - 1) % MRING
    return u * NITEM - 1 + i, (i - 1) % MRING


def interleave(first, ahead, lead):
    main = []
    for n in range(NST):
        main += [("scores", 0, (n, pair), 2 * COLS[n] + 2 * P * len(STEPS[n][1]) * (n in DIAG)) for pair in range(2)]
        if n >= LAG:
            main.append(("products", 0, n - LAG, 4 * COLS[n - LAG]))
        elif not first:
            main.append(("products", -1, NST + n - LAG, 4 * COLS[NST + n - LAG]))
    items = [(1, i) for i in range(LEAD, NITEM)] if ahead else []
    items += [(2, i) for i in (range(LEAD) if lead else [ROWS_AT])] if ahead else []
    cost = [PARTS_COST if i == ROWS_AT else MAXT[i - (i > ROWS_AT)][2] * MAXT[i - (i > ROWS_AT)][4] + 64 for _, i in items]
    whole, done, out, spent = sum(m[3] for m in main) * (1 if lead else LAST_PACE), 0, [], 0
    for m in main:
        out.append(m[:3])
        done += m[3]
        while items and (spent + cost[0] / 2) * whole <= done * (sum(cost) + spent):
            spent += cost.pop(0)
            out.append(("maximum", *items.pop(0)))
    return out + [("maximum", *x) for x in items]


def program(nc, x, w_qkv, b_qkv, w_out, b_out, w_gate, w_up, w_down, alibi, out):
    f32, f32r, bf16, f16 = mybir.dt.float32, mybir.dt.float32r, mybir.dt.bfloat16, mybir.dt.float16
    ALU, ACT, AX = mybir.AluOpType, mybir.ActivationFunctionType, mybir.AxisListType

    q_scr = nc.dram_tensor("q_scr", [B, 3, D, S], bf16, kind="Internal").ap()
    k_scr = nc.dram_tensor("k_scr", [B, 3, D, S], bf16, kind="Internal").ap()
    v_scr = nc.dram_tensor("v_scr", [T, D], f32, kind="Internal").ap()
    g_scr = nc.dram_tensor("g_scr", [T, D], f32, kind="Internal").ap()
    o_scr = nc.dram_tensor("o_scr", [B, 2, NQ, P, CH], f32, kind="Internal").ap()
    r_scr = nc.dram_tensor("r_scr", [B, 2, NQ, QH, CH], f32, kind="Internal").ap()

    xf = x.rearrange("b s d -> (b s) d")
    outf = out.rearrange("b s d -> (b s) d")

    top = ExitStack()
    with top:
        def alloc(stack, name, shape, dt):
            return stack.enter_context(nc.sbuf_tensor(name, shape, dt))

        def sem(name):
            return top.enter_context(nc.semaphore(name))

        psum = top.enter_context(nc.psum_tensor("psum", [P, 8, CH], f32))
        banks = [psum[:, i, :] for i in range(8)]
        identf = alloc(top, "identf", [P, P], f32)
        identb = alloc(top, "identb", [P, P], bf16)
        causal = alloc(top, "causal", [P, P], bf16)
        ones = alloc(top, "ones", [P, P], f32)
        primer = alloc(top, "primer", [P, 16], f32)
        OH = alloc(top, "OH", [P, KT, D], f32r)
        OL = alloc(top, "OL", [P, KT, D], f32r)

        X16 = alloc(top, "X16", [P, 2, KT, CH], f16)
        X16H, X16L = X16[:, 0], X16[:, 1]
        sig_scale = alloc(top, "sig_scale", [P, 1], f32)
        ffn_scale = alloc(top, "ffn_scale", [P, 1], f32)

        ffn = ExitStack()
        top.enter_context(ffn)
        MG = alloc(ffn, "MG", [P, KT, 2, HID], f16)
        MD = alloc(ffn, "MD", [P, HT, D], f16)
        hid = [alloc(ffn, f"hid{i}", [P, CH], f32) for i in range(NSIG)]
        g_stage = [alloc(ffn, f"g_stage{i}", [P, D], f32) for i in range(2)]
        shared = alloc(ffn, "shared", [P, HT * CH], f32)
        HHs = shared[:, 0:HT * CH // 2].bitcast(f16).rearrange("p (t n) -> p t n", t=HT)
        HLs = shared[:, HT * CH // 2:].bitcast(f16).rearrange("p (t n) -> p t n", t=HT)
        NG, ND = 2 * 2 * OC * DO, OC * HO
        GN = shared[0:GRP, 0:NG].rearrange("p (w g j d) -> p w g j d", w=2, g=2, j=OC)
        DN = shared[:, NG:NG + ND].rearrange("p (j d) -> p j d", j=OC)
        gtern = shared[0:GRP, NG + ND:NG + ND + NG // 2].bitcast(bf16).rearrange("p (w g j d) -> p w g j d", w=2, g=2, j=OC)
        dtern = shared[:, NG + ND + NG // 2:NG + ND + NG // 2 + ND // 2].bitcast(bf16).rearrange("p (j d) -> p j d", j=OC)

        s_const = sem("s_const")
        x_loaded = sem("x_loaded")
        x_tile_loaded = [sem(f"x_tile_loaded{i}") for i in range(TT)]
        w0_loaded = [sem(f"w0_loaded{i}") for i in range(KT)]
        w_loaded = [sem(f"w_loaded{i}") for i in range(4)]
        ffn_loaded = sem("ffn_loaded")
        bias_loaded = sem("bias_loaded")
        ln_step = sem("ln_step")
        std_done = sem("std_done")
        xt_done = sem("xt_done")
        xh_done = sem("xh_done")
        xl_done = sem("xl_done")
        wt_done = sem("wt_done")
        wh_done = sem("wh_done")
        wl_done = sem("wl_done")
        dve_prep = sem("dve_prep")
        asum_done = sem("asum_done")
        mean_ready = sem("mean_ready")
        tern_gu = sem("tern_gu")
        tern_dn = sem("tern_dn")
        tt_done = sem("tt_done")
        tt_copied = sem("tt_copied")
        mg_done = sem("mg_done")
        mdn_done = sem("mdn_done")
        mdt_done = sem("mdt_done")
        md_done = sem("md_done")
        tile_done = sem("tile_done")
        evac_done = sem("evac_done")
        q1_done = sem("q1_done")
        q2_done = sem("q2_done")
        q3_done = sem("q3_done")
        sig_done = sem("sig_done")
        hh_done = sem("hh_done")
        hl_done = sem("hl_done")
        qk_stored = [sem(f"qk_stored{i}") for i in range(2)]
        v_stored = [sem(f"v_stored{i}") for i in range(2)]
        g_stored = [sem(f"g_stored{i}") for i in range(2)]

        def evacuated(c, p):
            return c * TILES + TILES + p + 1

        def pe_gated(pe, c, bank, free, beside):
            for t in range(HT):
                for w in range(2):
                    p, n = GU0 + 2 * t + w, hidden_rows(t)
                    free(c, p)
                    for kt in range(KT):
                        wt = MG[:, kt, w, t * P:t * P + n]
                        nc.tensor.matmul(bank(p)[0:n], wt, X16H[:, kt, :], start=(kt == 0), stop=False)
                        last = nc.tensor.matmul(bank(p)[0:n], wt, X16L[:, kt, :], start=False, stop=(kt == KT - 1))
                    last.then_inc(tile_done, 1)
                    beside(p)
            for t in range(TT):
                p, tok = DN0 + t, slice(t * P, (t + 1) * P)
                free(c, p)
                for k in range(HT):
                    n = hidden_rows(k)
                    if t == 0:
                        pe.wait_ge(hl_done, c * HT + k + 1)
                    nc.tensor.matmul(bank(p), HHs[0:n, k, tok], MD[0:n, k, :], start=(k == 0), stop=False)
                    last = nc.tensor.matmul(bank(p), HLs[0:n, k, tok], MD[0:n, k, :], start=False, stop=(k == HT - 1))
                last.then_inc(tile_done, 1)
                beside(p)

        def act_gated(act, c, bank, beside):
            def high(t):
                n = hidden_rows(t)
                act.wait_ge(evac_done, evacuated(c, GU0 + 2 * t + 1))
                nc.scalar.activation(HHs[0:n, t, :], hid[t % NSIG][0:n], ACT.Identity).then_inc(hh_done, 1)

            for t in range(HT):
                p, n = GU0 + 2 * t, hidden_rows(t)
                act.wait_ge(tile_done, c * TILES + p + 1)
                if t >= NSIG:
                    act.wait_ge(hl_done, c * HT + t - NSIG + 1)
                nc.scalar.activation(hid[t % NSIG][0:n], bank(p)[0:n], ACT.Sigmoid, scale=sig_scale[0:n, 0:1]).then_inc(sig_done, 1)
                if t >= 1:
                    high(t - 1)
                beside(p)
            high(HT - 1)
            for t in range(TT):
                p = DN0 + t
                act.wait_ge(tile_done, c * TILES + p + 1)
                if t >= NSIG:
                    act.wait_ge(evac_done, evacuated(c, p - NSIG))
                nc.scalar.activation(hid[(HT + t) % NSIG][:], bank(p), ACT.Sigmoid, scale=ffn_scale[:, 0:1]).then_inc(sig_done, 1)
                beside(p)

        def dve_gated(dve, c, bank, beside):
            for t in range(HT):
                p, n, h = GU0 + 2 * t, hidden_rows(t), hid[t % NSIG]
                dve.wait_ge(sig_done, c * (HT + TT) + t + 1)
                nc.vector.tensor_tensor(h[0:n], bank(p)[0:n], h[0:n], ALU.mult).then_inc(evac_done, 1)
                beside(p)
                dve.wait_ge(tile_done, c * TILES + p + 2)
                dve.wait_ge(evac_done, evacuated(c, p))
                nc.vector.scalar_tensor_tensor(out=h[0:n], in0=bank(p + 1)[0:n], scalar=H_SCALE, in1=h[0:n],
                                               op0=ALU.mult, op1=ALU.mult).then_inc(evac_done, 1)
                beside(p + 1)
            for t in range(TT):
                dve.wait_ge(sig_done, c * (HT + TT) + HT + t + 1)
                dve.wait_ge(g_stored[t % 2], c * (TT // 2 * 16) + t // 2 * 16 + 16)
                nc.vector.scalar_tensor_tensor(out=g_stage[t % 2][:], in0=bank(DN0 + t), scalar=ffn_scale[:, 0:1],
                                               in1=hid[(HT + t) % NSIG][:], op0=ALU.mult, op1=ALU.mult).then_inc(evac_done, 1)
                beside(DN0 + t)

        def pool_gated(pool, c):
            for t in range(HT):
                n = hidden_rows(t)
                pool.wait_ge(hh_done, c * HT + t + 1)
                nc.gpsimd.tensor_tensor(HLs[0:n, t, :], hid[t % NSIG][0:n], HHs[0:n, t, :], ALU.subtract).then_inc(hl_done, 1)

        def sp_gated(sp, c):
            for t in range(TT):
                sp.wait_ge(evac_done, evacuated(c, DN0 + t))
                sp.dma_start(g_scr[bass.ds(c * CH + t * P, P), :], g_stage[t % 2][:]).then_inc(g_stored[t % 2], 16)

        one = ExitStack()
        with one:
            WH = alloc(one, "WH", [P, KT, 3 * D], f32r)
            WL = alloc(one, "WL", [P, KT, 3 * D], f32r)
            XH = alloc(one, "XH", [P, KT, CH], f32r)
            XL = alloc(one, "XL", [P, KT, CH], f32r)
            xin = alloc(one, "xin", [P, TT, D], f32)
            wnat = alloc(one, "wnat", [P, 2 * KT * D], f32)
            wraw = [wnat[:], MG[:].rearrange("p t w h -> p (t w h)").bitcast(f32)]
            wslot = [wraw[i // 2][:, i % 2 * KT * D:(i % 2 + 1) * KT * D].rearrange("p (t d) -> p t d", t=KT) for i in range(4)]
            NMDN = OC // 2 * ND
            MDn = wnat[:, 0:NMDN // 2].bitcast(bf16).rearrange("p (k i d) -> p k i d", k=OC // 2, i=OC)
            TTs = wnat[:, NMDN // 2:NMDN // 2 + ND].bitcast(bf16).rearrange("p (w j o) -> p w j o", w=2, j=OC)
            dneg = MDn[:, 0]
            gneg = TTs[0:GRP, 1].rearrange("p j o -> p (j o)")[:, 0:NG // 2]
            qk_stage = [alloc(one, f"qk_stage{i}", [P, 3, CH], bf16) for i in range(2)]
            rest = [alloc(one, f"rest{i}", [P, CH], f32) for i in range(2)]
            v_stage = [alloc(one, f"v_stage{i}", [P, D], f32) for i in range(2)]
            stats = alloc(one, "stats", [P, TT, 6], f32)
            moments = alloc(one, "moments", [P, TT, 2], f32)
            var_eps = alloc(one, "var_eps", [P, TT], f32)
            std = alloc(one, "std", [P, TT], f32)
            rstd0 = alloc(one, "rstd0", [P, TT], f32)
            rstd = alloc(one, "rstd", [P, TT], f32)
            newton = alloc(one, "newton", [P, 2, TT], f32)
            bq_col = alloc(one, "bq_col", [P, 2 * KT], f32)
            bv_row = alloc(one, "bv_row", [P, D], f32)
            asum = alloc(one, "asum", [P, 3], f32)
            mean = alloc(one, "mean", [P, 3], f32)
            half = alloc(one, "half", [P, 3], f32)
            nhalf = alloc(one, "nhalf", [P, 3], f32)
            gu_scale = alloc(one, "gu_scale", [P, 1], f32)

            NWT = 4 * KT
            NTT = 4
            ACT_DOWN = 6
            TT_AT = [2, 3]
            RING = 6

            def bank_of(p):
                return banks[2 + p % RING]

            def emptied(c, p):
                if p >= RING:
                    return evacuated(c, p - RING)
                before = max(b for b in range(TILES) if b % RING == p % RING)
                return c * TILES + before + 1

            def dve_normalise(dve, c, stage):
                base = c * LN_STEPS
                if stage == 0:
                    first = isinstance(c, int) and c == 0
                    if not first:
                        dve.wait_ge(x_loaded, c * 16)
                    for t in range(TT):
                        if first:
                            dve.wait_ge(x_tile_loaded[t], 16)
                        nc.vector.bn_stats(stats[:, t, :], xin[:, t, :]).then_inc(ln_step, 1)
                if stage == 1:
                    for t in range(TT):
                        nc.vector.bn_aggr(moments[:, t, :], stats[:, t, :]).then_inc(ln_step, 1)
                if stage == 2:
                    dve.wait_ge(ln_step, base + 8)
                    nc.vector.tensor_scalar(var_eps[:], moments[:, :, 1], EPS, None, ALU.add).then_inc(ln_step, 1)
                if stage == 3:
                    dve.wait_ge(std_done, c + 1)
                    nc.vector.reciprocal(rstd0[:], std[:]).then_inc(ln_step, 1)
                    dve.wait_ge(ln_step, base + 10)
                    nc.vector.tensor_tensor(newton[:, 0], var_eps[:], rstd0[:], ALU.mult).then_inc(ln_step, 1)
                    dve.wait_ge(ln_step, base + 11)
                    nc.vector.scalar_tensor_tensor(out=newton[:, 1], in0=newton[:, 0], scalar=-0.5, in1=rstd0[:],
                                                   op0=ALU.mult, op1=ALU.mult).then_inc(ln_step, 1)
                    dve.wait_ge(ln_step, base + 12)
                    nc.vector.scalar_tensor_tensor(out=rstd[:], in0=newton[:, 1], scalar=1.5, in1=rstd0[:],
                                                   op0=ALU.add, op1=ALU.mult).then_inc(ln_step, 1)
                if stage == 4:
                    dve.wait_ge(ln_step, base + 13)
                    for t in range(TT):
                        nc.vector.tensor_scalar(xin[:, t, :], xin[:, t, :], moments[:, t, 0:1], rstd[:, t:t + 1],
                                                ALU.subtract, ALU.mult).then_inc(ln_step, 1)

            def act_root(act, c):
                act.wait_ge(ln_step, c * LN_STEPS + 9)
                nc.scalar.activation(std[:], var_eps[:], ACT.Sqrt).then_inc(std_done, 1)

            def pe_transpose(pe, c, kt):
                if kt >= 2:
                    pe.wait_ge(xl_done, c * 2 * KT + 2 * (kt - 1))
                for t in range(TT):
                    last = nc.tensor.transpose(banks[kt % 2][:, t * P:(t + 1) * P], xin[:, t, kt * P:(kt + 1) * P], identf[:])
                last.then_inc(xt_done, 1)

            def act_split(act, c, kt):
                act.wait_ge(xt_done, c * KT + kt + 1)
                nc.scalar.activation(XH[:, kt, :], banks[kt % 2], ACT.Identity).then_inc(xh_done, 1)
                nc.scalar.activation(X16H[:, kt, :], banks[kt % 2], ACT.Identity, scale=X_SCALE).then_inc(xh_done, 1)

            def dve_split(dve, c, kt):
                dve.wait_ge(xh_done, c * 2 * KT + 2 * kt + 2)
                nc.vector.tensor_tensor(XL[:, kt, :], banks[kt % 2], XH[:, kt, :].bitcast(f32), ALU.subtract).then_inc(xl_done, 1)
                nc.vector.scalar_tensor_tensor(out=X16L[:, kt, :], in0=banks[kt % 2], scalar=X_SCALE, in1=X16H[:, kt, :],
                                               op0=ALU.mult, op1=ALU.subtract).then_inc(xl_done, 1)

            def weight(n):
                og, kt = divmod(n, KT)
                if og < 3:
                    return og, kt, WH[:, kt, og * D:(og + 1) * D], WL[:, kt, og * D:(og + 1) * D]
                return og, kt, OH[:, kt, :], OL[:, kt, :]

            def k_of(t):
                return (t * P + hidden_rows(t) - 1) // HO

            block = one.enter_context(nc.Block())

            @block.sync
            def _(sp):
                def load_weight(og):
                    src = w_qkv[og * D:(og + 1) * D, :] if og < 3 else w_out
                    sp.dma_start(wslot[og], src.rearrange("(t p) d -> p t d", p=P)).then_inc(w_loaded[og], 16)

                def store_qkv(c):
                    for m in range(2 * KT):
                        scr = q_scr if m < KT else k_scr
                        sp.wait_ge(q3_done, c * 2 * KT + m + 1)
                        sp.dma_start(scr[bass.ds(c // 2, 1), :, (m % KT) * P:(m % KT + 1) * P, bass.ds(c % 2 * CH, CH)].rearrange("a r p t -> p (a r) t"),
                                     qk_stage[m % 2][:]).then_inc(qk_stored[m % 2], 16)
                    for t in range(TT):
                        sp.wait_ge(evac_done, evacuated(c, V0 + t))
                        sp.dma_start(v_scr[bass.ds(c * CH + t * P, P), :], v_stage[t % 2][:]).then_inc(v_stored[t % 2], 16)

                def chunk(c):
                    sp.wait_ge(xt_done, c * KT + KT)
                    sp.dma_start(xin[:], xf[bass.ds((c + 1) * CH, CH), :].rearrange("(t p) d -> p t d", p=P)).then_inc(x_loaded, 16)
                    store_qkv(c)
                    sp_gated(sp, c)

                for t in range(TT):
                    sp.dma_start(xin[:, t, :], xf[t * P:(t + 1) * P, :]).then_inc(x_tile_loaded[t], 16)
                for kt in range(KT):
                    sp.dma_start(wslot[0][:, :, kt * P:(kt + 1) * P], w_qkv[0:D, kt * P:(kt + 1) * P].rearrange("(t p) d -> p t d", p=P)
                                 ).then_inc(w0_loaded[kt], 16)
                load_weight(1)
                for w, src in enumerate((w_gate, w_up)):
                    for g in range(2):
                        sp.dma_start(GN[:, w, g], src[:, g * GRP:(g + 1) * GRP, :].rearrange("j p d -> p j d")
                                       ).then_inc(ffn_loaded, 16)
                for r in range(2):
                    sp.dma_start(DN[DO * r:DO * (r + 1)], w_down.rearrange("j o d -> o j d")).then_inc(ffn_loaded, 16)
                for og in range(2, 4):
                    load_weight(og)
                with sp.Fori(0, LAST) as c:
                    chunk(c)
                store_qkv(LAST)
                for i in range(2):
                    sp.wait_ge(qk_stored[i], NCH * KT * 16 + 16)
                    sp.wait_ge(v_stored[i], NCH * TT // 2 * 16 + 16)

            @block.gpsimd
            def _(pool):
                nc.gpsimd.memset(identf[:], 0.0).then_inc(s_const, 1)
                nc.gpsimd.memset(identb[:], 0.0).then_inc(s_const, 1)
                nc.gpsimd.memset(causal[:], 0.0).then_inc(s_const, 1)
                nc.gpsimd.memset(ones[:], 1.0).then_inc(s_const, 1)
                pool.wait_ge(s_const, 4)
                nc.gpsimd.affine_select(out=identf[:], in_=identf[:], compare_op=ALU.not_equal, fill=1.0, base=0,
                                        pattern=[[-1, P]], channel_multiplier=1).then_inc(s_const, 1)
                nc.gpsimd.affine_select(out=identb[:], in_=identb[:], compare_op=ALU.not_equal, fill=1.0, base=0,
                                        pattern=[[-1, P]], channel_multiplier=1).then_inc(s_const, 1)
                nc.gpsimd.affine_select(out=causal[:], in_=causal[:], compare_op=ALU.is_ge, fill=MASKED, base=0,
                                        pattern=[[-1, P]], channel_multiplier=1).then_inc(s_const, 1)
                pool.dma_start(bq_col[:], b_qkv[0:2 * D].rearrange("(t p) -> p t", p=P),
                               allow_slow_non_contiguous=True).then_inc(bias_loaded, 16)
                pool.dma_start(bv_row[:], b_qkv[2 * D:3 * D].partition_broadcast(P)).then_inc(bias_loaded, 16)
                nc.gpsimd.memset(primer[:, 0:1], 0.0).then_inc(evac_done, TILES)
                for i in range(2):
                    for n, ring in enumerate((qk_stored, v_stored, g_stored)):
                        nc.gpsimd.memset(primer[:, 1 + 3 * i + n:2 + 3 * i + n], 0.0).then_inc(ring[i], 16)

                def third(c):
                    for m in range(2 * KT):
                        pool.wait_ge(q2_done, c * 2 * KT + m + 1)
                        nc.gpsimd.tensor_tensor(qk_stage[m % 2][:, 2, :], rest[m % 2][:], qk_stage[m % 2][:, 1, :],
                                                ALU.subtract).then_inc(q3_done, 1)

                third(0)
                pool.wait_ge(mdn_done, OC * OC)
                pool_gated(pool, 0)
                with pool.Fori(1, LAST) as c:
                    third(c)
                    pool_gated(pool, c)
                third(LAST)

            @block.scalar
            def _(act):
                def first(c, behind=lambda m: None):
                    for m in range(2 * KT):
                        act.wait_ge(tile_done, c * TILES + QK0 + m + 1)
                        act.wait_ge(qk_stored[m % 2], c * (KT * 16) + m // 2 * 16 + 16)
                        nc.scalar.activation(qk_stage[m % 2][:, 0, :], bank_of(QK0 + m), ACT.Identity,
                                             bias=bq_col[:, m:m + 1]).then_inc(q1_done, 1)
                        behind(m)

                def copy_ternary(n):
                    w, jq = divmod(n, 2)
                    act.wait_ge(tt_done, n + 1)
                    src = banks[n % 2].bitcast(bf16)[:, 0:OC * (GRP + 1)].rearrange("p (j g o) -> p j g o", g=2, o=GRP + 1)
                    nc.scalar.activation(TTs[:, w, jq * (OC // 2):(jq + 1) * (OC // 2), :].rearrange("p j (g o) -> p j g o", g=2),
                                         src[:, :, :, 0:GRP], ACT.Identity).then_inc(tt_copied, 1)

                def place_down(i):
                    for k in range(OC):
                        j, sign = OCT[k][i]
                        rows = slice(DO * (k % 2), DO * (k % 2 + 1))
                        nc.scalar.mul(MDn[rows, k // 2, i, :], dtern[rows, j, :], sign).then_inc(mdn_done, 1)

                def behind_first(m):
                    if m in TT_AT:
                        for n in range(2):
                            copy_ternary(2 * TT_AT.index(m) + n)
                    if m == KT:
                        act.wait_ge(tern_dn, 1)
                    if m >= KT:
                        place_down(m - KT)

                def beside_of(c):
                    def beside(p):
                        if p == GU0 + 2 * (LN_AT[2] + 1):
                            act_root(act, c + 1)
                        if DN0 <= p < DN0 + 2:
                            act_split(act, c + 1, 2 * (p - DN0))
                            act_split(act, c + 1, 2 * (p - DN0) + 1)
                    return beside

                def high_weight(n):
                    act.wait_ge(wt_done, n + 1)
                    nc.scalar.activation(weight(n)[2], banks[2 + n % RING], ACT.Identity).then_inc(wh_done, 1)

                act_root(act, 0)
                for n in range(KT):
                    high_weight(n)
                for kt in range(KT):
                    act_split(act, 0, kt)
                act.wait_ge(ffn_loaded, 6 * 16)
                act.wait_ge(asum_done, 1)
                for w in range(2):
                    nc.scalar.activation(gtern[:, w].rearrange("p g j d -> p (g j d)"), GN[:, w].rearrange("p g j d -> p (g j d)"), ACT.Abs,
                                         accum_out=asum[0:GRP, w:w + 1]).then_inc(asum_done, 1)
                nc.scalar.activation(dtern[0:DO].rearrange("p j d -> p (j d)"), DN[0:DO].rearrange("p j d -> p (j d)"), ACT.Abs,
                                     accum_out=asum[0:DO, 2:3]).then_inc(asum_done, 1)
                for n in range(KT, NWT):
                    high_weight(n)
                act.wait_ge(bias_loaded, 32)
                first(0, behind_first)
                for i in range(KT, ACT_DOWN):
                    place_down(i)
                later = beside_of(0)

                def beside(p):
                    t = (p - GU0) // 2
                    if GU0 <= p < DN0:
                        if t >= 1:
                            copy_down(t - 1)
                        if t == HT - 1:
                            copy_down(t)
                    later(p)

                def copy_down(m):
                    rows = hidden_rows(m)
                    act.wait_ge(mdt_done, m + 1)
                    nc.scalar.activation(MD[0:rows, m, :], banks[m % 2][0:rows].bitcast(bf16)[:, 0:D], ACT.Identity).then_inc(md_done, 1)

                act_gated(act, 0, bank_of, beside)
                with act.Fori(1, LAST) as c:
                    first(c)
                    act_gated(act, c, bank_of, beside_of(c))
                first(LAST)

            @block.vector
            def _(dve):
                chain = [0]

                def link(ins):
                    chain[0] += 1
                    ins.then_inc(dve_prep, 1)
                    dve.wait_ge(dve_prep, chain[0])

                def qkv(c, behind=lambda m: None):
                    for m in range(2 * KT):
                        dve.wait_ge(q1_done, c * 2 * KT + m + 1)
                        nc.vector.scalar_tensor_tensor(out=rest[m % 2][:], in0=bank_of(QK0 + m), scalar=bq_col[:, m:m + 1],
                                                       in1=qk_stage[m % 2][:, 0, :], op0=ALU.add, op1=ALU.subtract).then_inc(evac_done, 1)
                        dve.wait_ge(evac_done, evacuated(c, QK0 + m))
                        nc.vector.tensor_copy(qk_stage[m % 2][:, 1, :], rest[m % 2][:]).then_inc(q2_done, 1)
                        behind(m)
                    for t in range(TT):
                        dve.wait_ge(tile_done, c * TILES + V0 + t + 1)
                        dve.wait_ge(v_stored[t % 2], c * (TT // 2 * 16) + t // 2 * 16 + 16)
                        nc.vector.tensor_tensor(v_stage[t % 2][:].rearrange("p (q d h) -> p q h d", q=NQ, h=QH),
                                                bank_of(V0 + t).rearrange("p (q h d) -> p q h d", q=NQ, h=QH),
                                                bv_row[:].rearrange("p (q h d) -> p q h d", q=NQ, h=QH), ALU.add).then_inc(evac_done, 1)

                def beside_of(c):
                    def beside(p):
                        if GU0 <= p < DN0:
                            t, up = divmod(p - GU0, 2)
                            if up and t in LN_AT:
                                dve_normalise(dve, c + 1, LN_AT.index(t))
                            if not up and t == LN_AT[1]:
                                dve.wait_ge(ln_step, (c + 1) * LN_STEPS + 4)
                        if DN0 <= p < DN0 + 2:
                            dve_split(dve, c + 1, 2 * (p - DN0))
                            dve_split(dve, c + 1, 2 * (p - DN0) + 1)
                    return beside

                nc.vector.memset(asum[:], 0.0).then_inc(asum_done, 1)
                for stage in range(5):
                    if stage == 1:
                        dve.wait_ge(ln_step, 4)
                    dve_normalise(dve, 0, stage)
                def low_weight(n):
                    dve.wait_ge(wh_done, n + 1)
                    og, kt, hi, lo = weight(n)
                    nc.vector.tensor_tensor(lo, banks[2 + n % RING], hi.bitcast(f32), ALU.subtract).then_inc(wl_done, 1)

                for n in range(KT):
                    low_weight(n)
                for kt in range(KT):
                    dve_split(dve, 0, kt)
                for n in range(KT, NWT):
                    low_weight(n)
                dve.wait_ge(mean_ready, 1)
                link(nc.vector.tensor_scalar(mean[:], banks[0][:, 0:3], 1.0 / (OC * HO * DO), None, ALU.mult))
                nc.vector.tensor_scalar(half[:], mean[:], 0.5, None, ALU.mult)
                nc.vector.tensor_scalar(sig_scale[:], mean[:, 0:1], 1.0 / X_SCALE, None, ALU.mult)
                link(nc.vector.tensor_tensor(gu_scale[:], mean[:, 0:1], mean[:, 1:2], ALU.mult))
                link(nc.vector.tensor_scalar(ffn_scale[:], gu_scale[:], mean[:, 2:3], 1.0 / (X_SCALE * X_SCALE * H_SCALE), ALU.mult, ALU.mult))
                link(nc.vector.tensor_scalar(nhalf[:], mean[:], -0.5, None, ALU.mult))
                for w in range(2):
                    if w:
                        dve.wait_ge(tern_gu, w)
                    link(nc.vector.tensor_scalar(gneg, GN[:, w].rearrange("p g j d -> p (g j d)"), nhalf[0:GRP, w:w + 1], None, ALU.is_lt))
                    nc.vector.scalar_tensor_tensor(out=gtern[:, w].rearrange("p g j d -> p (g j d)"),
                                                   in0=GN[:, w].rearrange("p g j d -> p (g j d)"), scalar=half[0:GRP, w:w + 1], in1=gneg,
                                                   op0=ALU.is_gt, op1=ALU.subtract).then_inc(tern_gu, 1)
                dve.wait_ge(bias_loaded, 32)

                def place_gate_up(k):
                    for i in range(OC):
                        j, sign = OCT[k][i]
                        rows = slice(DO * (i % 2), DO * (i % 2 + 1))
                        last = nc.vector.tensor_scalar(MG[rows, i // 2, :, k * HO:(k + 1) * HO], TTs[rows, :, j, :], sign, None, ALU.mult)
                    last.then_inc(mg_done, 1)

                def place_down(i):
                    for k in range(OC):
                        j, sign = OCT[k][i]
                        rows = slice(DO * (k % 2), DO * (k % 2 + 1))
                        nc.vector.tensor_scalar(MDn[rows, k // 2, i, :], dtern[rows, j, :], sign, None, ALU.mult).then_inc(mdn_done, 1)

                def behind(m):
                    if m == 1:
                        link(nc.vector.tensor_scalar(dneg, DN, nhalf[:, 2:3], None, ALU.is_lt))
                        nc.vector.scalar_tensor_tensor(out=dtern, in0=DN, scalar=half[:, 2:3], in1=dneg,
                                                       op0=ALU.is_gt, op1=ALU.subtract).then_inc(tern_dn, 1)
                    if m == KT:
                        dve.wait_ge(tt_copied, NTT)
                    if m >= KT:
                        place_gate_up(2 * (m - KT))
                        place_gate_up(2 * (m - KT) + 1)
                    if m == 2 * KT - 1:
                        for i in range(ACT_DOWN, OC):
                            place_down(i)

                qkv(0, behind)
                dve_gated(dve, 0, bank_of, beside_of(0))
                with dve.Fori(1, LAST) as c:
                    qkv(c)
                    dve_gated(dve, c, bank_of, beside_of(c))
                qkv(LAST)

            @block.tensor
            def _(pe):
                def free(c, p):
                    pe.wait_ge(evac_done, emptied(c, p))

                def qk(c, behind=lambda m: None):
                    pe.wait_ge(xl_done, c * 2 * KT + 2 * KT)
                    for m in range(2 * KT):
                        cols = slice(m * P, (m + 1) * P)
                        free(c, QK0 + m)
                        for kt in range(KT):
                            nc.tensor.matmul(bank_of(QK0 + m), WH[:, kt, cols], XH[:, kt, :], start=(kt == 0), stop=False)
                            nc.tensor.matmul(bank_of(QK0 + m), WH[:, kt, cols], XL[:, kt, :], start=False, stop=False)
                            last = nc.tensor.matmul(bank_of(QK0 + m), WL[:, kt, cols], XH[:, kt, :], start=False, stop=(kt == KT - 1))
                        last.then_inc(tile_done, 1)
                        behind(m)

                def v(c):
                    for t in range(TT):
                        tok, cols = slice(t * P, (t + 1) * P), slice(2 * D, 3 * D)
                        free(c, V0 + t)
                        for kt in range(KT):
                            nc.tensor.matmul(bank_of(V0 + t), XH[:, kt, tok], WH[:, kt, cols], start=(kt == 0), stop=False)
                            nc.tensor.matmul(bank_of(V0 + t), XH[:, kt, tok], WL[:, kt, cols], start=False, stop=False)
                            last = nc.tensor.matmul(bank_of(V0 + t), XL[:, kt, tok], WH[:, kt, cols], start=False, stop=(kt == KT - 1))
                        last.then_inc(tile_done, 1)

                def beside_of(c):
                    def beside(p):
                        if p == DN0:
                            pe.wait_ge(ln_step, c * LN_STEPS + 2 * LN_STEPS)
                        if DN0 <= p < DN0 + 2:
                            pe_transpose(pe, c + 1, 2 * (p - DN0))
                            pe_transpose(pe, c + 1, 2 * (p - DN0) + 1)
                    return beside

                pe.wait_ge(s_const, 7)

                def transpose_weight(n):
                    og, kt, _, _ = weight(n)
                    if og == 0:
                        pe.wait_ge(w0_loaded[kt], 16)
                    elif kt == 0:
                        pe.wait_ge(w_loaded[og], 16)
                    if n >= RING:
                        pe.wait_ge(wl_done, n - RING + 1)
                    for t in range(TT):
                        last = nc.tensor.transpose(banks[2 + n % RING][:, t * P:(t + 1) * P], wslot[og][:, t, kt * P:(kt + 1) * P], identf[:])
                    last.then_inc(wt_done, 1)

                for n in range(KT):
                    transpose_weight(n)
                pe.wait_ge(ln_step, LN_STEPS)
                for kt in range(KT):
                    pe_transpose(pe, 0, kt)
                for n in range(KT, NWT):
                    transpose_weight(n)
                    if n == 3 * KT:
                        pe.wait_ge(asum_done, 4)
                        pe.wait_ge(xl_done, 2 * KT)
                        nc.tensor.matmul(banks[0][:, 0:3], ones[:], asum[:], start=True, stop=True).then_inc(mean_ready, 1)
                pe.wait_ge(wl_done, NWT)

                def transpose_ternary(m):
                    if m not in TT_AT:
                        return
                    pe.wait_ge(tern_gu, 2)
                    for n in range(2 * TT_AT.index(m), 2 * TT_AT.index(m) + 2):
                        w, jq = divmod(n, 2)
                        if n >= 2:
                            pe.wait_ge(tt_copied, n - 1)
                        dst = banks[n % 2].bitcast(bf16)
                        for jj in range(OC // 2):
                            for g in range(2):
                                at = (jj * 2 + g) * (GRP + 1)
                                for r in range(2):
                                    last = nc.tensor.transpose(dst[DO * r:DO * (r + 1), at:at + GRP],
                                                               gtern[:, w, g, jq * (OC // 2) + jj, :], identb[0:GRP, 0:GRP])
                        last.then_inc(tt_done, 1)

                qk(0, transpose_ternary)
                v(0)

                mdn = MDn.rearrange("p k i d -> p k (i d)")
                later = beside_of(0)

                def transpose_down(m):
                    if m >= 2:
                        pe.wait_ge(md_done, m - 1)
                    dst = banks[m % 2].bitcast(bf16)
                    for k in range(OC // 2):
                        last = nc.tensor.transpose(dst[0:hidden_rows(m), k * P:(k + 1) * P],
                                                   mdn[:, k, m * P:m * P + hidden_rows(m)], identb[:])
                    last.then_inc(mdt_done, 1)

                def beside(p):
                    if GU0 <= p < DN0:
                        t, up = divmod(p - GU0, 2)
                        if not up and t + 1 < HT:
                            pe.wait_ge(mg_done, k_of(t + 1) + 1)
                        if up:
                            if t == 0:
                                pe.wait_ge(mdn_done, OC * OC)
                            transpose_down(t)
                            if t == HT - 1:
                                pe.wait_ge(md_done, HT)
                    later(p)

                pe.wait_ge(mg_done, k_of(0) + 1)
                pe_gated(pe, 0, bank_of, free, beside)
                with pe.Fori(1, LAST) as c:
                    qk(c)
                    v(c)
                    pe_gated(pe, c, bank_of, free, beside_of(c))
                qk(LAST)
                v(LAST)

        two = ExitStack()
        with two:
            ffn.close()
            AH = [alloc(two, f"AH{i}", [P, KT, CH], f32r) for i in range(2)]
            AL = [alloc(two, f"AL{i}", [P, KT, CH], f32r) for i in range(2)]
            chunk_room = [alloc(two, f"chunk_room{i}", [P, KT, CH], f32) for i in range(4)]
            bo_row = alloc(two, "bo_row", [P, D], f32)
            den = alloc(two, "den", [P, NCH, P], f32)
            Qs = [alloc(two, f"Qs{i}", [P, QH, S], bf16) for i in range(SLOTS)]
            Ks = [alloc(two, f"Ks{i}", [P, QH, S], bf16) for i in range(SLOTS)]
            Vs = [alloc(two, f"Vs{i}", [P, KB, 2 * QH * HD], f32) for i in range(SLOTS)]
            probs = [alloc(two, f"probs{i}", [P, QH, CH], f32) for i in range(PSLOTS - 1)]
            probs.append(X16[:].rearrange("p a k t -> p (a k t)").bitcast(f32).rearrange("p (h t) -> p h t", h=QH))
            mx = [alloc(two, f"mx{i}", [P, QH, KB], f32) for i in range(2)]
            mx2 = [alloc(two, f"mx2{i}", [P, QH, KB // 2], f32) for i in range(2)]
            mrest = alloc(two, "mrest", [P, QH * KB], f32)
            mparts = alloc(two, "mparts", [P, 3, QH * KB], bf16)
            mrows = alloc(two, "mrows", [3 * QH * KB, P], bf16)
            osum = [alloc(two, f"osum{i}", [P, CH], f32) for i in range(2)]

            late = [x[i][:].rearrange("p h t -> p (h t)").bitcast(f32).rearrange("p (k t) -> p k t", k=KT) for i in LATE for x in (Qs, Ks)]
            last = [x[(QUADS - 1) % SLOTS][:].rearrange("p h t -> p (h t)").bitcast(f32).rearrange("p (k t) -> p k t", k=KT) for x in (Qs, Ks)]
            num = [chunk_room[0][:], chunk_room[1][:], chunk_room[2][:], probs[2][:]]
            rec = late[2:4]
            gate = late[0:2] + last
            v_room = [Vs[i][:].rearrange("p k c -> p (k c)").rearrange("p (t d) -> p t d", d=D) for i in LATE]
            xhalf = [[x[:, t:t + 2, :] for t in (0, 2)] for x in (chunk_room[3], probs[0], probs[1])]
            xhalf.insert(1, v_room)
            xres = [[x[t // 2][:, t % 2, :] for t in range(TT)] for x in xhalf]

            q_ones = sem("q_ones")
            v_ones = sem("v_ones")
            stacked = [sem(f"stacked{i}") for i in range(SLOTS)]
            max_filled = sem("max_filled")
            max_read = sem("max_read")
            max_step = sem("max_step")
            m_stacked = sem("m_stacked")
            s_filled = sem("s_filled")
            exp_done = sem("exp_done")
            pv_done = sem("pv_done")
            o_copied = sem("o_copied")
            o_stored = [sem(f"o_stored{i}") for i in range(2)]

            bo_loaded = sem("bo_loaded")
            den_loaded = sem("den_loaded")
            den_done = sem("den_done")
            rec_stored = sem("rec_stored")
            num_loaded = [sem(f"num_loaded{i}") for i in range(NCH)]
            rec_loaded = [sem(f"rec_loaded{i}") for i in range(2)]
            tok_loaded = [sem(f"tok_loaded{i}") for i in range(NCH)]
            att_done = sem("att_done")
            ah_done = sem("ah_done")
            al_done = sem("al_done")
            proj_done = sem("proj_done")
            proj_read = sem("proj_read")
            gated_done = sem("gated_done")
            fin_done = sem("fin_done")
            last_done = sem("last_done")
            fin_stored = sem("fin_stored")

            NLOAD = 2 * len(TERM_Q) + 2
            MSTEP = 5
            s_bank = [psum[:, 0:2, :], psum[:, 2:4, :]]
            m_bank = [banks[4], banks[5], banks[7]]
            pv_bank = banks[6]
            gated_banks = [banks[i] for i in (0, 1, 2, 3, 6)]
            FRING = len(gated_banks)
            early = [(0, i) for i in range(NITEM) if i != ROWS_AT] + [(1, i) for i in range(LEAD)]
            EARLY_FROM, EARLY_GU, EARLY_DN = 6, 3, 5

            def gated_bank(p):
                return gated_banks[(p - GU0) % FRING]

            def early_beside(p):
                def before(p):
                    gu = min(max(p - GU0 - EARLY_FROM, 0), 2 * HT - EARLY_FROM)
                    return gu * EARLY_GU + max(p - DN0, 0) * EARLY_DN
                return early[before(p):] if p == TILES - 1 else early[before(p):before(p + 1)]

            def stack_uses(t, s):
                return ((t - s) // SLOTS + 1) * NLOAD * 16

            block = two.enter_context(nc.Block())

            @block.sync
            def _(sp):
                def load(t, s, free):
                    if free:
                        sp.wait_ge(s_filled, (t - SLOTS) * (2 * NST) + 2 * NST)
                    b, hq = t // NQ, t % NQ
                    for n, (qp, kp) in enumerate(zip(TERM_Q, TERM_K)):
                        rows = slice(n * HD, (n + 1) * HD)
                        for dst, scr, part in ((Qs, q_scr, qp), (Ks, k_scr, kp)):
                            sp.dma_start(dst[s][rows], scr[bass.ds(b, 1), part, bass.ds(hq * (QH * HD), QH * HD)].rearrange("a (h d) t -> d (a h) t", d=HD)
                                         ).then_inc(stacked[s], 16)
                    sp.dma_start(Ks[s][ROWS_QK:ROWS_ALL], alibi[bass.ds(hq * QH, QH)].rearrange("h r t -> r h t")).then_inc(stacked[s], 16)
                    if free:
                        sp.wait_ge(pv_done, (t - SLOTS) * NST + NST + PSLOTS)
                    sp.dma_start(Vs[s][:, :, 0:QH * HD], v_scr[bass.ds(b * S, S), bass.ds(hq * (QH * HD), QH * HD)].rearrange("(k p) c -> p k c", p=P)
                                 ).then_inc(stacked[s], 16)

                def maximum(t, s):
                    sp.wait_ge(max_read, position(t + 1, ROWS_AT)[0] + 1 + MRING)
                    sp.dma_start(Qs[s][ROWS_MAX:ROWS_ALL], mrows[:]).then_inc(m_stacked, 16)

                def store(t, c):
                    sp.wait_ge(o_copied, t * 2 + c + 1)
                    sp.dma_start(o_scr[bass.ds(t // NQ, 1), c, bass.ds(t % NQ, 1)].rearrange("a b p t -> p (a b) t"), osum[c][:]
                                 ).then_inc(o_stored[c], 16)

                def step(t, s, ahead, lead):
                    if lead:
                        load(t + 2, (s + 2) % SLOTS, True)
                    store(t - 1, 1)
                    store(t, 0)
                    if ahead:
                        maximum(t + 1, (s + 1) % SLOTS)

                for i in range(SLOTS):
                    sp.dma_start(Qs[i][ROWS_QK:ROWS_MAX], alibi[0:QH, ROWS_MAX - ROWS_QK:].rearrange("h r t -> r h t")).then_inc(q_ones, 16)
                for i in range(SLOTS):
                    load(i, i, False)
                maximum(0, 0)
                sp_gated(sp, LAST)
                store(0, 0)
                maximum(1, 1)
                with sp.Fori(0, (QUADS - 4) // SLOTS) as g:
                    for s in range(SLOTS):
                        step(g * SLOTS + s + 1, (s + 1) % SLOTS, True, True)
                step(QUADS - 3, LATE[0], True, True)

                def denominators(c):
                    src = o_scr[c // 2, c % 2].rearrange("q (h x d) t -> x d (q h) t", x=2, d=HD)[1, 0]
                    sp.dma_start(den[:, c, :], src.rearrange("n (a t) -> n a t", t=P)).then_inc(den_loaded, 16)

                def inverted(c):
                    sp.wait_ge(den_done, c + 1)
                    sp.dma_start(r_scr[c // 2, c % 2].rearrange("q h (a t) -> (q h) a t", t=P), den[:, c, :]).then_inc(rec_stored, 16)

                def reciprocals(c):
                    sp.wait_ge(rec_stored, c * 16 + 16)
                    if c >= 2:
                        sp.wait_ge(att_done, (c - 1) * KT)
                    for kt in range(KT):
                        src = r_scr[c // 2, c % 2, 2 * kt:2 * kt + 2].rearrange("u h t -> (u h) t").unsqueeze(1)
                        sp.dma_start(rec[c % 2][:, kt], src.to_broadcast([2 * QH, HD, CH])).then_inc(rec_loaded[c % 2], 16)

                def sums(c):
                    for kt in range(KT):
                        src = o_scr[c // 2, c % 2, 2 * kt:2 * kt + 2].rearrange("u (h x d) t -> x (u h) d t", x=2, d=HD)
                        sp.dma_start(num[c][:, kt], src[0]).then_inc(num_loaded[c], 16)

                def gates(c):
                    sp.dma_start(gate[c], g_scr[c * CH:(c + 1) * CH, :].rearrange("(t p) d -> p t d", p=P)).then_inc(tok_loaded[c], 16)

                def residuals(c):
                    for t in range(0, TT, 2):
                        src = xf[c * CH + t * P:c * CH + (t + 2) * P, :].rearrange("(t p) d -> p t d", p=P)
                        sp.dma_start(xhalf[c][t // 2], src).then_inc(tok_loaded[c], 16)

                for c in range(2):
                    sp.wait_ge(o_stored[c], NQ * 16 + 16)
                    sp.wait_ge(g_stored[c], NCH * TT // 2 * 16 + 16)
                sp.dma_start(bo_row[:], b_out.partition_broadcast(P)).then_inc(bo_loaded, 16)
                for c in range(2):
                    denominators(c)
                for c in range(2):
                    sums(c)
                residuals(0)
                step(QUADS - 2, LATE[1], True, False)
                sp.wait_ge(s_filled, (QUADS - 1) * (2 * NST))
                inverted(0)
                reciprocals(0)
                store(QUADS - 2, 1)
                inverted(1)
                reciprocals(1)
                gates(0)
                gates(1)
                store(QUADS - 1, 0)
                sp.wait_ge(pv_done, (QUADS - 1) * NST + PSLOTS)
                residuals(1)
                sp.wait_ge(o_stored[0], QUADS * 16 + 16)
                denominators(2)
                sums(2)
                store(QUADS - 1, 1)
                inverted(2)
                sp.wait_ge(o_stored[1], QUADS * 16 + 16)
                denominators(3)
                reciprocals(2)
                sums(3)
                inverted(3)
                reciprocals(3)
                for c in range(2, NCH):
                    gates(c)
                    residuals(c)
                for c in range(NCH):
                    for t in range(TT):
                        if c < NCH - 1:
                            sp.wait_ge(fin_done, c * TT + t + 1)
                        else:
                            sp.wait_ge(last_done, t + 1)
                        sp.dma_start(outf[c * CH + t * P:c * CH + (t + 1) * P, :], xres[c][t]).then_inc(fin_stored, 16)
                sp.wait_ge(fin_stored, NCH * TT * 16)

            @block.gpsimd
            def _(pool):
                for n, (ring, count) in enumerate(((exp_done, 2), (max_read, MRING), (pv_done, PSLOTS), (m_stacked, 16),
                                                   (o_stored[0], 16), (o_stored[1], 16))):
                    nc.gpsimd.memset(primer[:, n:n + 1], 0.0).then_inc(ring, count)
                for i in range(SLOTS):
                    nc.gpsimd.memset(Vs[i][:, :, QH * HD:], 1.0).then_inc(v_ones, 1)
                pool_gated(pool, LAST)
                for c in range(NCH - 1):
                    for t in range(TT):
                        pool.wait_ge(gated_done, c * TT + t + 1)
                        nc.gpsimd.tensor_tensor(xres[c][t], gate[c][:, t, :], xres[c][t], ALU.add).then_inc(fin_done, 1)

            @block.scalar
            def _(act):
                def step(t, first, beside=lambda n: None):
                    for n in range(NST):
                        for pair in range(2):
                            act.wait_ge(s_filled, t * (2 * NST) + 2 * n + pair + 1)
                            act.wait_ge(pv_done, t * NST + n + 1)
                            nc.scalar.activation(probs[n % PSLOTS][:, 2 * pair:2 * pair + 2, 0:COLS[n]], s_bank[pair][:, :, 0:COLS[n]],
                                                 ACT.Exp, scale=1.0 / INV_SCALE).then_inc(exp_done, 1)
                        if n == LAG - 1 and not first:
                            copy_out(t - 1, 1, ENDS[1])
                        if n == ENDS[0] + LAG:
                            copy_out(t, 0, ENDS[0])
                        beside(n)

                def copy_out(t, c, n):
                    act.wait_ge(pv_done, t * NST + n + 1 + PSLOTS)
                    act.wait_ge(o_stored[c], t * 16 + 16)
                    nc.scalar.activation(osum[c][:], pv_bank, ACT.Copy).then_inc(o_copied, 1)

                act_gated(act, LAST, gated_bank, lambda p: None)
                def high(c):
                    if c >= 2:
                        act.wait_ge(proj_done, (c - 1) * TT)
                    for kt in range(KT):
                        act.wait_ge(att_done, c * KT + kt + 1)
                        nc.scalar.activation(AH[c % 2][:, kt, :], num[c][:, kt, :], ACT.Copy).then_inc(ah_done, 1)

                step(0, True)
                with act.Fori(0, (QUADS - 2) // 2) as g:
                    for i in range(2):
                        step(g * 2 + i + 1, False)
                step(QUADS - 1, False, lambda n: high(0) if n == NST - 2 else None)
                copy_out(QUADS - 1, 1, ENDS[1])
                for c in range(1, NCH):
                    high(c)

            @block.vector
            def _(dve):
                def read_max(t, i, s):
                    at, bank = position(t, i)
                    dve.wait_ge(max_filled, at + 1)
                    if i == ROWS_AT:
                        dve.wait_ge(m_stacked, t * 16)
                        nc.vector.tensor_copy(mrows[:], m_bank[bank][0:3 * QH * KB, 0:P // 2].bitcast(bf16)).then_inc(max_read, 1)
                        return
                    qb, h, n, k0, keys = MAXT[i - (i > ROWS_AT)]
                    dst = mx[s][:, h:h + n, qb:qb + 1] if k0 == 0 else mx2[s][:, h:h + n, qb - 4:qb - 3]
                    nc.vector.tensor_reduce(dst, m_bank[bank][:, 0:n * keys].rearrange("p (n k) -> p n k", n=n), AX.X, ALU.max
                                            ).then_inc(max_read, 1)

                def parts(t, s):
                    dve.wait_ge(max_read, position(t, NITEM - 1)[0] + 1 + MRING)
                    nc.vector.tensor_tensor(mx[s][:, :, 4:8], mx[s][:, :, 4:8], mx2[s][:], ALU.max).then_inc(max_step, 1)
                    flat = mx[s][:].rearrange("p h q -> p (h q)")
                    dve.wait_ge(max_step, t * MSTEP + 1)
                    nc.vector.tensor_scalar(mparts[:, 0, :], flat, -1.0, None, ALU.mult).then_inc(max_step, 1)
                    dve.wait_ge(max_step, t * MSTEP + 2)
                    nc.vector.scalar_tensor_tensor(out=mrest[:], in0=flat, scalar=-1.0, in1=mparts[:, 0, :], op0=ALU.mult,
                                                   op1=ALU.subtract).then_inc(max_step, 1)
                    dve.wait_ge(max_step, t * MSTEP + 3)
                    nc.vector.tensor_copy(mparts[:, 1, :], mrest[:]).then_inc(max_step, 1)
                    dve.wait_ge(max_step, t * MSTEP + 4)
                    nc.vector.tensor_tensor(mparts[:, 2, :], mrest[:], mparts[:, 1, :], ALU.subtract).then_inc(max_step, 1)

                def beside(p):
                    for t, i in early_beside(p):
                        read_max(t, i, t)
                        if (t, i) == (0, NITEM - 1):
                            parts(0, 0)

                dve_gated(dve, LAST, gated_bank, beside)
                for i in range(LEAD, NITEM):
                    read_max(1, i, 1)
                parts(1, 1)
                with dve.Fori(1, QUADS // 2) as g:
                    for s in range(2):
                        for i in range(NITEM):
                            read_max(g * 2 + s, i, s)
                        parts(g * 2 + s, s)
                read_max(QUADS, ROWS_AT, 0)

                def invert(c):
                    dve.wait_ge(den_loaded, max(c + 1, 2) * 16)
                    nc.vector.reciprocal(den[:, c, :], den[:, c, :]).then_inc(den_done, 1)

                def normalise(c):
                    dve.wait_ge(num_loaded[c], KT * 16)
                    dve.wait_ge(rec_loaded[c % 2], (c // 2 + 1) * KT * 16)
                    for kt in range(KT):
                        nc.vector.tensor_tensor(num[c][:, kt, :], num[c][:, kt, :], rec[c % 2][:, kt, :], ALU.mult).then_inc(att_done, 1)

                def low(c):
                    if c >= 2:
                        dve.wait_ge(proj_done, (c - 1) * TT)
                    for kt in range(KT):
                        dve.wait_ge(ah_done, c * KT + kt + 1)
                        nc.vector.tensor_tensor(AL[c % 2][:, kt, :], num[c][:, kt, :], AH[c % 2][:, kt, :].bitcast(f32), ALU.subtract
                                                ).then_inc(al_done, 1)

                def finish(c):
                    dve.wait_ge(tok_loaded[c], (1 + TT // 2) * 16)
                    for t in range(TT):
                        n = c * TT + t
                        dve.wait_ge(proj_done, n + 1)
                        if n >= 2:
                            dve.wait_ge(gated_done, n - 1)
                        nc.vector.tensor_tensor(osum[t % 2][:], banks[TT * (c % 2) + t], bo_row[:], ALU.add).then_inc(proj_read, 1)
                        dve.wait_ge(proj_read, n + 1)
                        nc.vector.tensor_tensor(gate[c][:, t, :], osum[t % 2][:], gate[c][:, t, :], ALU.mult).then_inc(gated_done, 1)
                        if c == NCH - 1:
                            dve.wait_ge(gated_done, n + 1)
                            nc.vector.tensor_tensor(xres[c][t], gate[c][:, t, :], xres[c][t], ALU.add).then_inc(last_done, 1)

                invert(0)
                invert(1)
                dve.wait_ge(bo_loaded, 16)
                normalise(0)
                low(0)
                normalise(1)
                invert(2)
                low(1)
                invert(3)
                for c in range(2):
                    dve.wait_ge(o_stored[c], QUADS * 16 + 16)
                for c in range(NCH):
                    finish(c)
                    if c + 2 < NCH:
                        normalise(c + 2)
                        low(c + 2)

            @block.tensor
            def _(pe):
                def fill_max(t, i, s):
                    at, bank = position(t, i)
                    if i == 0:
                        if isinstance(t, int) and t == 0:
                            pe.wait_ge(q_ones, SLOTS * 16)
                        pe.wait_ge(stacked[s], stack_uses(t, s))
                    pe.wait_ge(max_read, at + 1)
                    if i == ROWS_AT:
                        pe.wait_ge(max_step, t * MSTEP)
                        nc.tensor.transpose(m_bank[bank][0:3 * QH * KB, 0:P // 2].bitcast(bf16), mparts[:].rearrange("p r n -> p (r n)"), identb[:]
                                            ).then_inc(max_filled, 1)
                        return
                    qb, h, n, k0, keys = MAXT[i - (i > ROWS_AT)]
                    masked = k0 + keys == (qb + 1) * P
                    tile = m_bank[bank][:, 0:n * keys].rearrange("p (n k) -> p n k", n=n)
                    for hh in range(n):
                        last = nc.tensor.matmul(tile[:, hh, :], Qs[s][0:ROWS_MAX, h + hh, qb * P:(qb + 1) * P], Ks[s][0:ROWS_MAX, h + hh, k0:k0 + keys],
                                                start=(hh == 0), stop=not masked and hh == n - 1)
                    if masked:
                        last = nc.tensor.matmul(tile[:, :, keys - P:], identb[:], causal[:].unsqueeze(1).to_broadcast([P, n, P]), start=False, stop=True)
                    last.then_inc(max_filled, 1)

                def scores(t, n, pair, s):
                    c, blocks = STEPS[n]
                    pe.wait_ge(exp_done, t * (2 * NST) + 2 * n + pair + 1)
                    for h in range(2):
                        bank = s_bank[pair][:, h, :]
                        for kb, at, cols in blocks:
                            last = nc.tensor.matmul(bank[:, at:at + cols], Ks[s][0:ROWS_ALL, 2 * pair + h, kb * P:(kb + 1) * P],
                                                    Qs[s][0:ROWS_ALL, 2 * pair + h, (c + 1) * CH - cols:(c + 1) * CH], start=(at == 0), stop=n not in DIAG)
                        if n in DIAG:
                            squares = bank.rearrange("p (a q) -> p a q", q=P)[:, 0:blocks[-1][1] // P + 1:max(blocks[-1][1] // P, 1)]
                            last = nc.tensor.matmul(squares, causal[:], identb[:].unsqueeze(1).to_broadcast([P, len(blocks), P]), start=False, stop=True)
                    last.then_inc(s_filled, 1)

                def products(t, n, s):
                    c, blocks = STEPS[n]
                    pe.wait_ge(exp_done, t * (2 * NST) + 2 * n + 2 + 2)
                    if blocks[0][0] == 0 and not (isinstance(t, int) and t == 0 and c == 0):
                        pe.wait_ge(o_copied, t * 2 + c)
                    for kb, at, cols in blocks:
                        for h in range(QH):
                            last = nc.tensor.matmul(pv_bank[32 * h:32 * h + 32, CH - cols:CH], Vs[s][:, kb, h::QH],
                                                    probs[n % PSLOTS][:, h, at:at + cols], start=(kb == 0), stop=(kb == 4 * c + 3))
                    last.then_inc(pv_done, 1)

                def step(t, s, ahead, lead):
                    pe.wait_ge(m_stacked, t * 16 + 32)
                    for kind, a, b in interleave(isinstance(t, int) and t == 0, ahead, lead):
                        if kind == "scores":
                            scores(t, *b, s)
                        elif kind == "products":
                            products(t + a, b, (s + a) % SLOTS)
                        else:
                            fill_max(t + a, b, (s + a) % SLOTS)

                def free(c, p):
                    if p - GU0 >= FRING:
                        pe.wait_ge(evac_done, evacuated(c, p - FRING))

                def beside(p):
                    for t, i in early_beside(p):
                        fill_max(t, i, t)

                pe_gated(pe, LAST, gated_bank, free, beside)
                pe.wait_ge(evac_done, evacuated(LAST, TILES - 1))
                pe.wait_ge(v_ones, SLOTS)
                step(0, 0, True, True)
                with pe.Fori(0, (QUADS - 4) // SLOTS) as g:
                    for s in range(SLOTS):
                        step(g * SLOTS + s + 1, (s + 1) % SLOTS, True, True)
                step(QUADS - 3, LATE[0], True, True)
                step(QUADS - 2, LATE[1], True, False)
                step(QUADS - 1, (QUADS - 1) % SLOTS, False, False)
                for n in range(NST - LAG, NST):
                    products(QUADS - 1, n, (QUADS - 1) % SLOTS)
                for c in range(NCH):
                    if c == 1:
                        pe.wait_ge(o_copied, 2 * QUADS)
                        pe.wait_ge(max_read, position(QUADS, ROWS_AT)[0] + 1 + MRING)
                    pe.wait_ge(al_done, c * KT + KT)
                    high, low = AH[c % 2], AL[c % 2]
                    for t in range(TT):
                        tok, bank = slice(t * P, (t + 1) * P), banks[TT * (c % 2) + t]
                        if c >= 2:
                            pe.wait_ge(proj_read, (c - 2) * TT + t + 1)
                        for kt in range(KT):
                            nc.tensor.matmul(bank, high[:, kt, tok], OH[:, kt, :], start=(kt == 0), stop=False)
                            nc.tensor.matmul(bank, high[:, kt, tok], OL[:, kt, :], start=False, stop=False)
                            last = nc.tensor.matmul(bank, low[:, kt, tok], OH[:, kt, :], start=False, stop=(kt == KT - 1))
                        last.then_inc(proj_done, 1)


def alibi_parts():
    import numpy as np

    m = np.arange(1, H + 1, dtype=np.float32) * np.float32(8 / H)
    slopes = np.float32(1.0) / np.power(np.float32(2.0), m)
    rest = slopes[:, None] * np.arange(1 - S, 1, dtype=np.float32)[None, :] * np.float32(INV_SCALE)
    parts = []
    for _ in range(3):
        bits = rest.view(np.uint32) & np.uint32(0xFFFF0000)
        parts.append((bits >> 16).astype(np.uint16))
        rest = rest - bits.view(np.float32)
    parts += [np.full((H, S), 0x3F80, np.uint16)] * 3
    return np.ascontiguousarray(np.stack(parts, axis=1))


_INS = ["L0_attn_x", "L0_attn_w_qkv", "L0_attn_b_qkv", "L0_attn_w_out", "L0_attn_b_out", "L0_ffn_w_gate", "L0_ffn_w_up", "L0_ffn_w_down"]


def kernel(**inputs):
    import numpy as np
    import concourse.bacc as bacc
    from concourse.bass_utils import run_bass_kernel_spmd

    nc = bacc.Bacc("TRN2", target_bir_lowering=False, num_devices=1)
    arrays = {f"in_{name}": np.ascontiguousarray(inputs[name]) for name in _INS}
    args = [nc.dram_tensor(n, a.shape, mybir.dt.from_np(a.dtype), kind="ExternalInput").ap() for n, a in arrays.items()]
    arrays["alibi"] = alibi_parts()
    alibi = nc.dram_tensor("alibi", arrays["alibi"].shape, mybir.dt.uint16, kind="ExternalInput").ap().bitcast(mybir.dt.bfloat16)
    out = nc.dram_tensor("out", (B, S, D), mybir.dt.float32, kind="ExternalOutput").ap()
    program(nc, *args, alibi, out)
    r = run_bass_kernel_spmd(nc, [arrays], core_ids=[0])
    return r.results[0]["out"]
```
